# Optimizing a Trainium2 kernel written in Bass

```python
import numpy as np
import jax
import jax.numpy as jnp

def _softmax(x, axis=-1):
    return jax.nn.softmax(x, axis=axis)

def _gelu(x):
    return jax.nn.gelu(x, approximate=True)

def _silu(x):
    return jax.nn.silu(x)

def _sigmoid(x):
    return jax.nn.sigmoid(x)

def _layernorm(x, axis=-1, eps=1e-05):
    m = jnp.mean(x, axis=axis, keepdims=True)
    v = jnp.var(x, axis=axis, keepdims=True)
    return (x - m) / jnp.sqrt(v + eps)

def _scatter_add(tgt, idx, src, axis=0):
    return tgt.at[idx].add(src)

def _segment_sum(src, seg, n):
    return jax.ops.segment_sum(src, seg, n)
kernel_name = 'mk_seq_preln_d1_jaxref_r8_0c5eb3'

def setup_inputs(seed: int=0):
    np.random.seed(seed)
    _w = jnp.asarray

    def _L0_attn_setup():
        import jax, jax.numpy as jnp
        import numpy as np
        WINDOW = 64

        def _block_local_attn(q, k, v, window):
            B, H, T, D = q.shape
            W = window
            nb = T // W
            scale = 1.0 / jnp.sqrt(jnp.asarray(D, q.dtype))
            qb = q.reshape(B, H, nb, W, D)
            kb = k.reshape(B, H, nb, W, D)
            vb = v.reshape(B, H, nb, W, D)
            kp = jnp.pad(kb, ((0, 0), (0, 0), (1, 0), (0, 0), (0, 0)))[:, :, :nb]
            vp = jnp.pad(vb, ((0, 0), (0, 0), (1, 0), (0, 0), (0, 0)))[:, :, :nb]
            k2 = jnp.concatenate([kp, kb], axis=3)
            v2 = jnp.concatenate([vp, vb], axis=3)
            i = jnp.arange(W)[:, None]
            j = jnp.arange(2 * W)[None, :]
            base = (j > i) & (j <= i + W)
            prev_ok = (jnp.arange(nb)[:, None] > 0) | (jnp.arange(2 * W)[None, :] >= W)
            mask = base[None, :, :] & prev_ok[:, None, :]
            scores = jnp.einsum('bhnqd,bhnkd->bhnqk', qb, k2) * scale
            scores = jnp.where(mask[None, None], scores, jnp.asarray(-1e+30, scores.dtype))
            p = jax.nn.softmax(scores, axis=-1)
            out = jnp.einsum('bhnqk,bhnkd->bhnqd', p, v2)
            return out.reshape(B, H, T, D)
        key = jax.random.key(seed)
        ks = jax.random.split(key, 5)
        B, T, C = (2, 1024, 128)
        s = 1.0 / np.sqrt(C)
        return {'x': jax.random.normal(ks[0], (B, T, C), dtype=jnp.float32), 'Wq': jax.random.normal(ks[1], (C, C), dtype=jnp.float32) * s, 'Wk': jax.random.normal(ks[2], (C, C), dtype=jnp.float32) * s, 'Wv': jax.random.normal(ks[3], (C, C), dtype=jnp.float32) * s, 'Wo': jax.random.normal(ks[4], (C, C), dtype=jnp.float32) * s}
    _L0_attn_in = _L0_attn_setup()

    def _L0_ffn_setup():
        import jax, jax.numpy as jnp
        import numpy as np
        H = 128
        M = 64
        E = 16
        TOP_K = 4
        N_GROUP = 4
        TOPK_GROUP = 2
        SCALE = 2.5
        B, S = (2, 128)

        def _gate(x2d, gate_kernel, gate_bias):
            n = x2d.shape[0]
            logits = jnp.dot(x2d.astype(jnp.float32), gate_kernel.astype(jnp.float32))
            scores = jax.nn.sigmoid(logits)
            scores_for_choice = scores + gate_bias
            group_scores = scores_for_choice.reshape(n, N_GROUP, E // N_GROUP)
            top2 = jax.lax.top_k(group_scores, k=2)[0]
            group_sum = jnp.sum(top2, axis=-1)
            group_idx = jax.lax.top_k(group_sum, k=TOPK_GROUP)[1]
            group_mask = jnp.zeros_like(group_sum).at[jnp.arange(n)[:, None], group_idx].set(1.0)
            score_mask = jnp.repeat(group_mask[:, :, None], E // N_GROUP, axis=2).reshape(n, E)
            masked_scores = jnp.where(score_mask > 0, scores_for_choice, 0.0)
            topk_weight, topk_idx = jax.lax.top_k(masked_scores, k=TOP_K)
            topk_weight = topk_weight / (jnp.sum(topk_weight, axis=-1, keepdims=True) + 1e-20)
            topk_weight = topk_weight * SCALE
            return (topk_idx, topk_weight)
        key = jax.random.key(seed)
        ks = jax.random.split(key, 9)
        sc_h = 1.0 / np.sqrt(H)
        sc_m = 1.0 / np.sqrt(M)
        return {'hidden_states': jax.random.normal(ks[0], (B, S, H), jnp.float32), 'gate_kernel': jax.random.normal(ks[1], (H, E), jnp.float32) * sc_h, 'gate_bias': jax.random.normal(ks[2], (E,), jnp.float32) * 0.01, 'w_gate': jax.random.normal(ks[3], (E, H, M), jnp.float32) * sc_h, 'w_up': jax.random.normal(ks[4], (E, H, M), jnp.float32) * sc_h, 'w_down': jax.random.normal(ks[5], (E, M, H), jnp.float32) * sc_m, 'sw_gate': jax.random.normal(ks[6], (H, 2 * M), jnp.float32) * sc_h, 'sw_up': jax.random.normal(ks[7], (H, 2 * M), jnp.float32) * sc_h, 'sw_down': jax.random.normal(ks[8], (2 * M, H), jnp.float32) * (1.0 / np.sqrt(2 * M))}
    _L0_ffn_in = _L0_ffn_setup()
    _d = {'L0_attn_x': _L0_attn_in['x'], 'L0_attn_Wq': _L0_attn_in['Wq'], 'L0_attn_Wk': _L0_attn_in['Wk'], 'L0_attn_Wv': _L0_attn_in['Wv'], 'L0_attn_Wo': _L0_attn_in['Wo'], 'L0_ffn_gate_kernel': _L0_ffn_in['gate_kernel'], 'L0_ffn_gate_bias': _L0_ffn_in['gate_bias'], 'L0_ffn_w_gate': _L0_ffn_in['w_gate'], 'L0_ffn_w_up': _L0_ffn_in['w_up'], 'L0_ffn_w_down': _L0_ffn_in['w_down'], 'L0_ffn_sw_gate': _L0_ffn_in['sw_gate'], 'L0_ffn_sw_up': _L0_ffn_in['sw_up'], 'L0_ffn_sw_down': _L0_ffn_in['sw_down']}
    _x0 = _d['L0_attn_x']
    _d['L0_attn_x'] = jax.random.normal(jax.random.fold_in(jax.random.key(seed), 1), (32, 256, 128), dtype=_x0.dtype)
    del _x0
    return _d

def reference(L0_attn_x, L0_attn_Wq, L0_attn_Wk, L0_attn_Wv, L0_attn_Wo, L0_ffn_gate_kernel, L0_ffn_gate_bias, L0_ffn_w_gate, L0_ffn_w_up, L0_ffn_w_down, L0_ffn_sw_gate, L0_ffn_sw_up, L0_ffn_sw_down):

    def _L0_attn_ref(x, Wq, Wk, Wv, Wo):
        import jax, jax.numpy as jnp
        import numpy as np
        WINDOW = 64

        def _block_local_attn(q, k, v, window):
            B, H, T, D = q.shape
            W = window
            nb = T // W
            scale = 1.0 / jnp.sqrt(jnp.asarray(D, q.dtype))
            qb = q.reshape(B, H, nb, W, D)
            kb = k.reshape(B, H, nb, W, D)
            vb = v.reshape(B, H, nb, W, D)
            kp = jnp.pad(kb, ((0, 0), (0, 0), (1, 0), (0, 0), (0, 0)))[:, :, :nb]
            vp = jnp.pad(vb, ((0, 0), (0, 0), (1, 0), (0, 0), (0, 0)))[:, :, :nb]
            k2 = jnp.concatenate([kp, kb], axis=3)
            v2 = jnp.concatenate([vp, vb], axis=3)
            i = jnp.arange(W)[:, None]
            j = jnp.arange(2 * W)[None, :]
            base = (j > i) & (j <= i + W)
            prev_ok = (jnp.arange(nb)[:, None] > 0) | (jnp.arange(2 * W)[None, :] >= W)
            mask = base[None, :, :] & prev_ok[:, None, :]
            scores = jnp.einsum('bhnqd,bhnkd->bhnqk', qb, k2) * scale
            scores = jnp.where(mask[None, None], scores, jnp.asarray(-1e+30, scores.dtype))
            p = jax.nn.softmax(scores, axis=-1)
            out = jnp.einsum('bhnqk,bhnkd->bhnqd', p, v2)
            return out.reshape(B, H, T, D)
        B, T, C = x.shape
        H = 16
        D = C // H
        q = (x @ Wq.T).reshape(B, T, H, D).transpose(0, 2, 1, 3)
        k = (x @ Wk.T).reshape(B, T, H, D).transpose(0, 2, 1, 3)
        v = (x @ Wv.T).reshape(B, T, H, D).transpose(0, 2, 1, 3)
        out = _block_local_attn(q, k, v, WINDOW)
        out = out.transpose(0, 2, 1, 3).reshape(B, T, C)
        return out @ Wo.T

    def _L0_ffn_ref(hidden_states, gate_kernel, gate_bias, w_gate, w_up, w_down, sw_gate, sw_up, sw_down):
        import jax, jax.numpy as jnp
        import numpy as np
        H = 128
        M = 64
        E = 16
        TOP_K = 4
        N_GROUP = 4
        TOPK_GROUP = 2
        SCALE = 2.5
        B, S = (2, 128)

        def _gate(x2d, gate_kernel, gate_bias):
            n = x2d.shape[0]
            logits = jnp.dot(x2d.astype(jnp.float32), gate_kernel.astype(jnp.float32))
            scores = jax.nn.sigmoid(logits)
            scores_for_choice = scores + gate_bias
            group_scores = scores_for_choice.reshape(n, N_GROUP, E // N_GROUP)
            top2 = jax.lax.top_k(group_scores, k=2)[0]
            group_sum = jnp.sum(top2, axis=-1)
            group_idx = jax.lax.top_k(group_sum, k=TOPK_GROUP)[1]
            group_mask = jnp.zeros_like(group_sum).at[jnp.arange(n)[:, None], group_idx].set(1.0)
            score_mask = jnp.repeat(group_mask[:, :, None], E // N_GROUP, axis=2).reshape(n, E)
            masked_scores = jnp.where(score_mask > 0, scores_for_choice, 0.0)
            topk_weight, topk_idx = jax.lax.top_k(masked_scores, k=TOP_K)
            topk_weight = topk_weight / (jnp.sum(topk_weight, axis=-1, keepdims=True) + 1e-20)
            topk_weight = topk_weight * SCALE
            return (topk_idx, topk_weight)
        orig_shape = hidden_states.shape
        x = hidden_states.reshape(-1, orig_shape[-1])
        topk_idx, topk_weight = _gate(x, gate_kernel, gate_bias)
        onehot = (topk_idx[:, :, None] == jnp.arange(E)[None, None, :]).astype(topk_weight.dtype)
        combine = jnp.einsum('nke,nk->ne', onehot, topk_weight)
        g = jnp.einsum('nh,ehm->enm', x, w_gate)
        u = jnp.einsum('nh,ehm->enm', x, w_up)
        inter = jax.nn.silu(g) * u
        y_e = jnp.einsum('enm,emh->enh', inter, w_down)
        y = jnp.einsum('ne,enh->nh', combine, y_e)
        shared = jnp.dot(jax.nn.silu(jnp.dot(x, sw_gate)) * jnp.dot(x, sw_up), sw_down)
        return (y + shared).reshape(orig_shape)
    x = L0_attn_x
    x = x + _L0_attn_ref(_layernorm(x, axis=-1), L0_attn_Wq, L0_attn_Wk, L0_attn_Wv, L0_attn_Wo)
    x = x + _L0_ffn_ref(_layernorm(x, axis=-1), L0_ffn_gate_kernel, L0_ffn_gate_bias, L0_ffn_w_gate, L0_ffn_w_up, L0_ffn_w_down, L0_ffn_sw_gate, L0_ffn_sw_up, L0_ffn_sw_down)
    return x

_drawn_inputs = setup_inputs


def setup_inputs(seed=0):
    import zlib

    import numpy as np

    out = dict(_drawn_inputs(seed))
    spreads = {}
    factors = {}
    for name, (base, spread) in spreads.items():
        noise = np.random.default_rng([zlib.crc32(name.encode()), seed]).standard_normal(out[name].shape)
        drawn = base * np.exp(spread * noise) if base else spread * noise
        out[name] = jnp.asarray(drawn.astype(out[name].dtype))
    for name, factor in factors.items():
        out[name] = (out[name] * factor).astype(out[name].dtype)
    return out
```

```python
from contextlib import ExitStack

import concourse.bass as bass
from concourse import mybir

F32 = mybir.dt.float32
F32R = mybir.dt.float32r
BF16 = mybir.dt.bfloat16
ALU = mybir.AluOpType
ACT = mybir.ActivationFunctionType
AX_X = mybir.AxisListType.X

P = 128
B, T, C = 32, 256, 128
H, D, W = 16, 8, 64
E, M = 16, 64
TOP_K, N_GROUP, TOPK_GROUP, ROUTE_SCALE = 4, 4, 2, 2.5
EPS = 1e-5

GB = 4
NG = B // GB
TOK = GB * T
NT = TOK // P
NC = TOK // 512
Q = 32
NQ = T // Q
HG = P // (4 * D)
KW = W + Q
NU = GB * NQ // 2
NJ = E // 2 + 1
NK = NC * NJ
NCB = NC * (NJ - 1)
LAST_STEP = NU + 8

CONSTS = {"ident": P, "headrow": 4, "grouprow": 2, "headcol": 32, "lower": N_GROUP * N_GROUP,
          "unit": 8 * KW, "pick": (NJ - 1) * P, "band": KW, "ident4": P, "spreadq": 4 * P}
CONST_AT, CONST_COLS = {}, 0
for _name, _cols in CONSTS.items():
    CONST_AT[_name] = CONST_COLS
    CONST_COLS += _cols
KEPT = CONST_AT["unit"]

DVE_LINKS = 30


def preln_block_kernel(nc, x, wq, wk, wv, wo, gate_w, gate_b, w_gu, w_down, sw_down, consts, out):
    with ExitStack() as ctx:
        def sb(name, shape, dt=F32):
            return ctx.enter_context(nc.sbuf_tensor(name, shape, dt))

        def sem(name):
            return ctx.enter_context(nc.semaphore(name))

        cst = sb("cst", [P, KEPT])
        w_hi = sb("w_hi", [P, 4 * C + E + 2 * NJ * P], F32R)
        w_lo = sb("w_lo", [P, 4 * C + E + 2 * NJ * P], F32R)
        wd = sb("wd", [P, NJ, C])
        unit = sb("unit", [64, 8, KW], F32R)
        pick = sb("pick", [64, NJ - 1, P], F32R)
        band = sb("band", [P, KW], BF16)
        ident4 = sb("ident4", [P, P], BF16)
        zero_bf = sb("zero_bf", [1, 512], BF16)
        bias_b = sb("bias_b", [P, E])
        X = sb("X", [P, NT, C])
        stats = sb("stats", [P, NT, 6])
        mv = sb("mv", [P, NT, 2])
        holder = sb("holder", [P, 1])
        eps = sb("eps", [P, NT])
        veps = sb("veps", [P, NT])
        half_neg = sb("half_neg", [P, NT])
        rstd = sb("rstd", [P, NT])
        xn = sb("xn", [P, NT, C])
        xT_hi = sb("xT_hi", [P, TOK], F32R)
        xT_lo = sb("xT_lo", [P, TOK], F32R)
        q_hi = sb("q_hi", [P, TOK // Q, 4, Q], F32R)
        q_lo = sb("q_lo", [P, TOK // Q, 4, Q], F32R)
        k_hi = sb("k_hi", [P, 2, TOK], F32R)
        k_lo = sb("k_lo", [P, 2, TOK], F32R)
        v_hi = sb("v_hi", [P, NT, C], F32R)
        v_lo = sb("v_lo", [P, NT, C], F32R)
        spreadq = sb("spreadq", [P, 4, P], F32R)
        v_bd = sb("v_bd", [P, GB * NQ, HG, 2, 32])
        neg_max = sb("neg_max", [P, 2, 8])
        mT = sb("mT", [64, P], F32R)
        probs = sb("probs", [P, 2, 2, 2, 2, KW])
        probsT = sb("probsT", [P, 2, HG, NQ, 3, Q])
        spare = probsT[:, :, :, :, :, :].rearrange("p b g t c q -> p (b g t c q)")
        stage = spare[:, 0:4 * C + E + 2 * NJ * P]
        cst_stage = spare[:, 4 * C + E + 2 * NJ * P:4 * C + E + 2 * NJ * P + CONST_COLS - KEPT]
        o_f = sb("o_f", [P, 2, T])
        o_rs = sb("o_rs", [P, 8, 4])
        o_n = sb("o_n", [P, 2, P])
        oT_hi = sb("oT_hi", [P, T], F32R)
        oT_lo = sb("oT_lo", [P, T], F32R)
        H2 = sb("H2", [P, NT, C])
        th = sb("th", [P, NT * E])
        sc = sb("sc", [P, NT * E])
        pair = sb("pair", [P, NT * N_GROUP, 6])
        gs = sb("gs", [P, NT * N_GROUP])
        g_gt = sb("g_gt", [P, NT, N_GROUP, N_GROUP])
        g_eq = sb("g_eq", [P, NT, N_GROUP, N_GROUP])
        g_rank = sb("g_rank", [P, NT * N_GROUP])
        ms = sb("ms", [P, NT, E])
        m8 = sb("m8", [P, NT, 8])
        e_gt = sb("e_gt", [P, NT, E])
        e_eq = sb("e_eq", [P, NT, E])
        cum = sb("cum", [P, 2, NT, 8 + E])
        n_gt = sb("n_gt", [P, NT])
        w_sum = sb("w_sum", [P, NT])
        comb = sb("comb", [P, NT, E])
        cT = sb("cT", [64, TOK], F32R)
        sg = sb("sg", [P, 2, 512])
        hh = sb("hh", [P, 2, 512])
        y_f = sb("y_f", [P, 512])
        PS = ctx.enter_context(nc.psum_tensor("PS", [P, 8, 512], F32))

        def const(name, rows=P):
            if CONST_AT[name] >= KEPT:
                return cst_stage[0:rows, CONST_AT[name] - KEPT:CONST_AT[name] - KEPT + CONSTS[name]]
            return cst[0:rows, CONST_AT[name]:CONST_AT[name] + CONSTS[name]]

        ident = const("ident")
        grouprow = const("grouprow")
        headrow = const("headrow")
        headcol = const("headcol")
        lower = const("lower").rearrange("p (i j) -> p i j", i=N_GROUP)

        def weight(buf, n, cols=C):
            return buf[:, n:n + cols]

        WQ, WK, WV, WO, GK = 0, C, 2 * C, 3 * C, 4 * C
        WG = GK + E
        WU = WG + NJ * P

        s_w = sem("weights_loaded")
        s_cst = sem("constants_ready")
        s_x = sem("x_loaded")
        s_mv = sem("mean_var_ready")
        s_rs = sem("rstd_ready")
        s_pool = sem("pool_order")
        s_xn = sem("xn_ready")
        s_xt_ps = sem("xT_in_psum")
        s_xt_hi = sem("xT_hi_ready")
        s_xt_lo = sem("xT_lo_ready")
        s_q_ps = sem("q_in_psum")
        s_k_ps = sem("k_in_psum")
        s_q_hi = sem("q_hi_ready")
        s_q_lo = sem("q_lo_ready")
        s_k_hi = sem("k_hi_ready")
        s_k_lo = sem("k_lo_ready")
        s_vt_ps = sem("v_tokens_in_psum")
        s_v_hi = sem("v_hi_ready")
        s_v_lo = sem("v_lo_ready")
        s_v_ps = sem("v_in_psum")
        s_v = sem("v_ready")
        s_s = sem("scores_ready")
        s_m = sem("neg_max_ready")
        s_mt_ps = sem("mT_in_psum")
        s_mt_hi = sem("mT_hi_ready")
        s_mt = sem("mT_ready")
        s_sm = sem("scores_less_max")
        s_p = sem("probs_ready")
        s_pt = sem("probsT_ready")
        s_o_ps = sem("o_in_psum")
        s_o = sem("o_ready")
        s_ot_ps = sem("o_tokens_in_psum")
        s_on = sem("o_norm_ready")
        s_ont_ps = sem("oT_in_psum")
        s_ont_hi = sem("oT_hi_ready")
        s_ont = sem("oT_ready")
        s_y_ps = sem("attn_out_in_psum")
        s_h2 = sem("h2_ready")
        s_lg = sem("logits_in_psum")
        s_th = sem("tanh_ready")
        s_cb = sem("combine_ready")
        s_ct_ps = sem("cT_in_psum")
        s_ct_hi = sem("cT_hi_ready")
        s_ct = sem("cT_ready")
        s_g = sem("gate_in_psum")
        s_u = sem("up_in_psum")
        s_c = sem("weights_spread")
        s_si = sem("silu_ready")
        s_h1 = sem("silu_up_ready")
        s_h = sem("hidden_ready")
        s_hc = sem("spread_read")
        s_f = sem("ffn_ready")
        s_fo = sem("ffn_tokens_in_psum")
        s_out = sem("out_ready")
        s_st = sem("stored")
        s_dve = sem("dve_order")

        x_t = x.rearrange("(g n p) c -> g p n c", n=NT, p=P)
        out_t = out.rearrange("(g n p) c -> g p n c", n=NT, p=P)

        def hidden_done(eng, i, k):
            c, j = divmod(k, NJ)
            if j == NJ - 1:
                eng.wait_ge(s_h1, i * NK + k + 1)
            else:
                eng.wait_ge(s_h, i * NCB + c * (NJ - 1) + j + 1)

        block = ctx.enter_context(nc.Block())

        @block.sync
        def _(sp):
            sp.dma_start(X[:, :, :], x_t[0]).then_inc(s_x, 16)
            sp.dma_start(cst[:, :], consts[:, 0:KEPT]).then_inc(s_w, 16)
            sp.dma_start(cst_stage, consts[:, KEPT:CONST_COLS]).then_inc(s_w, 16)
            for n, w in ((WQ, wq), (WK, wk), (WV, wv), (WO, wo)):
                sp.dma_start(weight(stage, n), w).then_inc(s_w, 16)
            sp.dma_start(weight(stage, GK, E), gate_w).then_inc(s_w, 16)
            sp.dma_start(stage[:, WG:WG + 2 * NJ * P], w_gu).then_inc(s_w, 16)
            sp.dma_start(wd[:, 0:NJ - 1, :], w_down.rearrange("(j p) c -> p j c", p=P)).then_inc(s_w, 16)
            sp.dma_start(wd[:, NJ - 1, :], sw_down).then_inc(s_w, 16)
            sp.dma_start(bias_b[:, :], gate_b.partition_broadcast(P)).then_inc(s_w, 16)

            def store(i, c):
                sp.wait_ge(s_out, i * NC + c + 1)
                sp.dma_start(out_t[i, :, 4 * c:4 * c + 4, :], H2[:, 4 * c:4 * c + 4, :]).then_inc(s_st, 16)

            with sp.Fori(0, NG - 1) as i:
                sp.wait_ge(s_h2, i * NT + NT)
                sp.dma_start(X[:, :, :], x_t[i + 1]).then_inc(s_x, 16)
                for c in range(NC):
                    store(i, c)
            for c in range(NC):
                store(NG - 1, c)
            sp.wait_ge(s_st, 16 * NC * NG + 1)

        @block.gpsimd
        def _(pool):
            nc.gpsimd.memset(half_neg[:, :], -0.5).then_inc(s_pool, 1)
            nc.gpsimd.memset(eps[:, :], EPS).then_inc(s_pool, 1)
            pool.wait_ge(s_pool, 2)
            with pool.Fori(0, 2 * NG) as i:
                pool.wait_ge(s_mv, i + 1)
                nc.gpsimd.tensor_tensor(veps[:, :], mv[:, :, 1], eps[:, :], ALU.add).then_inc(s_pool, 1)
                pool.wait_ge(s_pool, i + 3)
                nc.gpsimd.tensor_tensor(rstd[:, :], veps[:, :], half_neg[:, :], ALU.pow).then_inc(s_rs, 1)

        @block.scalar
        def _(act):
            def copy(dst, src, **kw):
                return nc.scalar.activation(dst, src, ACT.Copy, **kw)

            act.wait_ge(s_w, 176)
            copy(w_hi[:, :], stage).then_inc(s_cst, 1)

            def xT_high(i, ln):
                for c in range(NC):
                    act.wait_ge(s_xt_ps, i * 2 * NC + ln * NC + c + 1)
                    copy(xT_hi[:, 512 * c:512 * c + 512], PS[:, c, :]).then_inc(s_xt_hi, 1)

            with act.Fori(0, NG) as i:
                xT_high(i, 0)
                for c in range(NC):
                    cols = slice(512 * c, 512 * c + 512)
                    act.wait_ge(s_q_ps, i * NC + c + 1)
                    for v in range(4):
                        ins = copy(q_hi[:, 16 * c:16 * c + 16, v, :], PS[:, 2 + c, :].rearrange("p (a q) -> p a q", q=Q),
                                   scale=headrow[:, v:v + 1])
                    ins.then_inc(s_q_hi, 1)
                    act.wait_ge(s_k_ps, i * NC + c + 1)
                    for e in range(2):
                        ins = copy(k_hi[:, e, cols], PS[:, 4 + c, :], scale=grouprow[:, e:e + 1])
                    ins.then_inc(s_k_hi, 1)
                for c in range(NC):
                    act.wait_ge(s_vt_ps, i * NC + c + 1)
                    copy(v_hi[:, 4 * c:4 * c + 4, :], PS[:, 6 + c, :].rearrange("p (n f) -> p n f", n=4)).then_inc(s_v_hi, 1)
                for s in range(LAST_STEP):
                    if 0 <= s - 2 < NU:
                        u = s - 2
                        act.wait_ge(s_sm, i * NU + u + 1)
                        if u >= 2:
                            act.wait_ge(s_pt, i * NU + u - 1)
                        j0 = Q if u % 4 == 0 else 0
                        src = PS[:, 2 * (u % 2):2 * (u % 2) + 2, 0:4 * KW].rearrange("p a (r k) -> p a r k", r=4)
                        ins = nc.scalar.activation(probs[:, u % 2, :, :, :, j0:KW].rearrange("p a t e k -> p a (t e) k"),
                                                   src[:, :, :, j0:KW], ACT.Exp, scale=float(D) ** -0.5)
                        ins.then_inc(s_p, 1)
                    if 0 <= s - 1 < NU:
                        u = s - 1
                        act.wait_ge(s_mt_ps, i * NU + u + 1)
                        if u >= 1:
                            act.wait_ge(s_sm, i * NU + u)
                        copy(mT[0:8, :], PS[0:8, 4, 0:P]).then_inc(s_mt_hi, 1)
                    b, at = divmod(s - 8, 4)
                    if 0 <= b < GB and at == 0:
                        act.wait_ge(s_o_ps, i * GB + b + 1)
                        if b >= 1:
                            act.wait_ge(s_ot_ps, i * GB + b)
                        copy(o_f[:, :, :], PS[:, 5 + b % 2, :].rearrange("p (j q) -> p j q", j=2)).then_inc(s_o, 1)
                    if 0 <= b < GB and at == 2:
                        act.wait_ge(s_ont_ps, i * GB + b + 1)
                        copy(oT_hi[:, :], PS[:, 7, 0:T]).then_inc(s_ont_hi, 1)
                xT_high(i, 1)
                act.wait_ge(s_lg, i + 1)
                nc.scalar.activation(th[:, :], PS[:, 7, 0:NT * E], ACT.Tanh, scale=0.5).then_inc(s_th, 1)

                def silu(k):
                    act.wait_ge(s_g, i * NK + k + 1)
                    if k >= 2:
                        hidden_done(act, i, k - 2)
                    nc.scalar.activation(sg[:, k % 2, :], PS[:, k % 2, :], ACT.Silu).then_inc(s_si, 1)

                silu(0)
                for c in range(NC):
                    act.wait_ge(s_ct_ps, i * NC + c + 1)
                    copy(cT[0:E, 512 * c:512 * c + 512], PS[0:E, 6 + c, :]).then_inc(s_ct_hi, 1)
                for k in range(1, NK):
                    silu(k)
                    if k % NJ == 0:
                        act.wait_ge(s_hc, i * NK + k)
                        copy(y_f[:, :], PS[:, 6, :]).then_inc(s_f, 1)
                act.wait_ge(s_hc, i * NK + NK)
                act.wait_ge(s_fo, i * NC + NC - 1)
                copy(y_f[:, :], PS[:, 6, :]).then_inc(s_f, 1)

        @block.vector
        def _(dve):
            v_ = nc.vector
            v_.memset(zero_bf[:, :], 0.0)
            v_.memset(holder[:, :], 0.0).then_inc(s_st, 1)
            v_.memset(mT[:, :].bitcast(F32), 0.0)
            v_.memset(cT[:, :].bitcast(F32), 0.0)
            v_.memset(cum[:, :, :, :], 0.0)
            dve.wait_ge(s_w, 176)
            for kb in range(GB * NQ):
                v_.tensor_copy(v_bd[:, kb, :, 1, :], headcol.unsqueeze(1).broadcast_to([P, HG, 32]))
            v_.tensor_copy(spreadq[:, :, :], const("spreadq").rearrange("p (a k) -> p a k", a=4))
            v_.tensor_copy(unit[:, :, :], const("unit", 64).rearrange("p (r k) -> p r k", r=8))
            v_.tensor_copy(pick[:, :, :], const("pick", 64).rearrange("p (j k) -> p j k", k=P))
            v_.tensor_copy(band[:, :], const("band"))
            v_.tensor_copy(ident4[:, :], const("ident4"))
            dve.wait_ge(s_cst, 1)
            v_.tensor_tensor(w_lo[:, :], stage, w_hi[:, :].bitcast(F32), ALU.subtract).then_inc(s_cst, 1)
            dve.wait_ge(s_cst, 2)

            with dve.Fori(0, NG) as i:
                links = [0]

                def link(ins):
                    links[0] += 1
                    ins.then_inc(s_dve, 1)
                    dve.wait_ge(s_dve, i * DVE_LINKS + links[0])

                def split_low(dst, src, high):
                    return v_.tensor_tensor(dst, src, high.bitcast(F32), ALU.subtract)

                def layernorm(src, ln):
                    for n in range(NT):
                        ins = v_.bn_stats(stats[:, n, :], src[:, n, :])
                    link(ins)
                    v_.memset(holder[:, :], 0.0)
                    for n in range(NT):
                        ins = v_.bn_aggr(mv[:, n, :], stats[:, n, :])
                    ins.then_inc(s_mv, 1)
                    dve.wait_ge(s_mv, i * 2 + ln + 1)
                    dve.wait_ge(s_rs, i * 2 + ln + 1)
                    for n in range(NT):
                        v_.tensor_scalar(xn[:, n, :], src[:, n, :], mv[:, n, 0:1], rstd[:, n:n + 1],
                                         ALU.subtract, ALU.mult).then_inc(s_xn, 1)

                def xT_low(ln):
                    for c in range(NC):
                        dve.wait_ge(s_xt_hi, i * 2 * NC + ln * NC + c + 1)
                        cols = slice(512 * c, 512 * c + 512)
                        split_low(xT_lo[:, cols], PS[:, c, :], xT_hi[:, cols]).then_inc(s_xt_lo, 1)

                dve.wait_ge(s_x, i * 16 + 16)
                layernorm(X, 0)
                xT_low(0)
                for c in range(NC):
                    cols = slice(512 * c, 512 * c + 512)
                    dve.wait_ge(s_q_hi, i * NC + c + 1)
                    for v in range(4):
                        blocks = slice(16 * c, 16 * c + 16)
                        ins = v_.scalar_tensor_tensor(q_lo[:, blocks, v, :],
                                                      PS[:, 2 + c, :].rearrange("p (a q) -> p a q", q=Q),
                                                      headrow[:, v:v + 1], q_hi[:, blocks, v, :].bitcast(F32),
                                                      ALU.mult, ALU.subtract)
                    ins.then_inc(s_q_lo, 1)
                    dve.wait_ge(s_k_hi, i * NC + c + 1)
                    for e in range(2):
                        ins = v_.scalar_tensor_tensor(k_lo[:, e, cols], PS[:, 4 + c, :], grouprow[:, e:e + 1],
                                                      k_hi[:, e, cols].bitcast(F32), ALU.mult, ALU.subtract)
                    ins.then_inc(s_k_lo, 1)
                for c in range(NC):
                    dve.wait_ge(s_v_hi, i * NC + c + 1)
                    split_low(v_lo[:, 4 * c:4 * c + 4, :], PS[:, 6 + c, :].rearrange("p (n f) -> p n f", n=4),
                              v_hi[:, 4 * c:4 * c + 4, :]).then_inc(s_v_lo, 1)
                for n in range(2 * GB):
                    c, a = divmod(n, 4)
                    dve.wait_ge(s_v_ps, i * 2 * GB + n + 1)
                    bank = (0, 1, 6, 7)[a]
                    v_.tensor_tensor(
                        v_bd[:, 16 * c + a:16 * c + a + 13:4, :, 0, :],
                        PS[:, bank, :].rearrange("p (n g f) -> p n g f", g=HG, f=32),
                        headcol.unsqueeze(1).unsqueeze(1).broadcast_to([P, 4, HG, 32]), ALU.mult).then_inc(s_v, 1)

                for s in range(LAST_STEP):
                    if 0 <= s - 2 < NU:
                        u = s - 2
                        b, t0 = u // 4, 2 * (u % 4)
                        dve.wait_ge(s_p, i * NU + u + 1)
                        if b >= 2 and u % 4 == 0:
                            dve.wait_ge(s_o_ps, i * GB + b - 1)
                        c0 = 1 if u % 4 == 0 else 0
                        for tt in range(2):
                            ins = v_.transpose(
                                probsT[:, b % 2, :, t0 + tt, c0:3, :].rearrange("p (a e) c q -> p a e (c q)", e=2),
                                probs[:, u % 2, :, tt, :, c0 * Q:KW])
                        ins.then_inc(s_pt, 1)
                    if 0 <= s - 1 < NU:
                        u = s - 1
                        dve.wait_ge(s_mt_hi, i * NU + u + 1)
                        split_low(mT[32:40, :], PS[0:8, 4, 0:P], mT[0:8, :]).then_inc(s_mt, 1)
                    if s < NU:
                        dve.wait_ge(s_s, i * NU + s + 1)
                        if s >= 2:
                            dve.wait_ge(s_mt_ps, i * NU + s - 1)
                        j0 = Q if s % 4 == 0 else 0
                        src = PS[:, 2 * (s % 2):2 * (s % 2) + 2, 0:4 * KW].rearrange("p a (r k) -> p a r k", r=4)
                        v_.tensor_reduce(neg_max[:, s % 2, :].rearrange("p (a r) -> p a r", a=2),
                                         src[:, :, :, j0:KW], AX_X, ALU.max, negate=True).then_inc(s_m, 1)
                    b, at = divmod(s - 8, 4)
                    if 0 <= b < GB and at == 1:
                        dve.wait_ge(s_ot_ps, i * GB + b + 1)
                        o_t = PS[:, 7, :].rearrange("p (a k v d) -> p a k v d", k=2, v=4, d=D)
                        link(v_.reciprocal(o_rs[:, :, :], o_t[:, :, 1, :, 0]))
                        v_.tensor_tensor(o_n[:, :, :].rearrange("p n (a v d) -> p (n a) v d", v=4, d=D),
                                         o_t[:, :, 0, :, :],
                                         o_rs[:, :, :].unsqueeze(3).broadcast_to([P, 8, 4, D]),
                                         ALU.mult).then_inc(s_on, 1)
                    if 0 <= b < GB and at == 2:
                        dve.wait_ge(s_ont_hi, i * GB + b + 1)
                        split_low(oT_lo[:, :], PS[:, 7, 0:T], oT_hi[:, :]).then_inc(s_ont, 1)
                    if 0 <= b < GB and at == 3:
                        dve.wait_ge(s_y_ps, i * GB + b + 1)
                        if b == 0:
                            dve.wait_ge(s_st, i * 16 * NC + 1)
                        v_.tensor_tensor(H2[:, 2 * b:2 * b + 2, :],
                                         PS[:, 7, T:2 * T].rearrange("p (n c) -> p n c", n=2),
                                         X[:, 2 * b:2 * b + 2, :], ALU.add).then_inc(s_h2, 2)

                dve.wait_ge(s_h2, i * NT + NT)
                layernorm(H2, 1)
                xT_low(1)

                dve.wait_ge(s_th, i + 1)
                link(v_.tensor_scalar(th[:, :], th[:, :], 0.5, 0.5, ALU.mult, ALU.add))
                link(v_.tensor_tensor(sc[:, :].rearrange("p (n e) -> p n e", n=NT),
                                      th[:, :].rearrange("p (n e) -> p n e", n=NT),
                                      bias_b[:, :].unsqueeze(1).broadcast_to([P, NT, E]), ALU.add))
                s4 = sc[:, :].rearrange("p (n e) -> p n e", e=4)
                v_.tensor_tensor(pair[:, :, 0:3], s4[:, :, 0:3], s4[:, :, 1:4], ALU.add)
                v_.tensor_tensor(pair[:, :, 3:5], s4[:, :, 0:2], s4[:, :, 2:4], ALU.add)
                link(v_.tensor_tensor(pair[:, :, 5:6], s4[:, :, 0:1], s4[:, :, 3:4], ALU.add))
                link(v_.tensor_reduce(gs[:, :], pair[:, :, :], AX_X, ALU.max))
                gs3 = gs[:, :].rearrange("p (n g) -> p n g", n=NT)
                g_j = gs3.unsqueeze(2).broadcast_to([P, NT, N_GROUP, N_GROUP])
                g_i = gs3.unsqueeze(3).broadcast_to([P, NT, N_GROUP, N_GROUP])
                v_.tensor_tensor(g_gt[:, :, :, :], g_j, g_i, ALU.is_gt)
                link(v_.tensor_tensor(g_eq[:, :, :, :], g_j, g_i, ALU.is_equal))
                link(v_.tensor_tensor(g_eq[:, :, :, :], g_eq[:, :, :, :],
                                      lower.unsqueeze(1).broadcast_to([P, NT, N_GROUP, N_GROUP]), ALU.mult))
                link(v_.tensor_tensor(g_gt[:, :, :, :], g_gt[:, :, :, :], g_eq[:, :, :, :], ALU.add))
                link(v_.tensor_reduce(g_rank[:, :], g_gt[:, :, :, :].rearrange("p n i j -> p (n i) j"), AX_X, ALU.add))
                link(v_.tensor_scalar(g_rank[:, :], g_rank[:, :], float(TOPK_GROUP), None, ALU.is_lt))
                link(v_.tensor_tensor(ms[:, :, :].rearrange("p n (g e) -> p (n g) e", g=N_GROUP), s4,
                                      g_rank[:, :].unsqueeze(2).broadcast_to([P, NT * N_GROUP, 4]), ALU.mult))
                v_.memset(holder[:, :], 0.0)
                for n in range(NT):
                    ins = v_.max(m8[:, n, :], ms[:, n, :])
                link(ins)
                fourth = m8[:, :, TOP_K - 1:TOP_K].broadcast_to([P, NT, E])
                v_.tensor_tensor(e_gt[:, :, :], ms[:, :, :], fourth, ALU.is_gt)
                v_.tensor_tensor(e_eq[:, :, :], ms[:, :, :], fourth, ALU.is_equal)
                link(v_.tensor_tensor(cum[:, 0, :, 8:8 + E], ms[:, :, :], fourth, ALU.is_equal))
                for n, d in enumerate((1, 2, 4, 8)):
                    a, z = n % 2, 1 - n % 2
                    link(v_.tensor_tensor(cum[:, z, :, 8:8 + E], cum[:, a, :, 8:8 + E], cum[:, a, :, 8 - d:8 + E - d],
                                          ALU.add))
                link(v_.tensor_reduce(n_gt[:, :], e_gt[:, :, :], AX_X, ALU.add))
                link(v_.tensor_tensor(cum[:, 1, :, 8:8 + E], cum[:, 0, :, 8:8 + E],
                                      n_gt[:, :].unsqueeze(2).broadcast_to([P, NT, E]), ALU.add))
                link(v_.scalar_tensor_tensor(e_eq[:, :, :], cum[:, 1, :, 8:8 + E], float(TOP_K), e_eq[:, :, :],
                                             ALU.is_le, ALU.mult))
                link(v_.tensor_tensor(e_gt[:, :, :], e_gt[:, :, :], e_eq[:, :, :], ALU.add))
                link(v_.tensor_tensor(ms[:, :, :], ms[:, :, :], e_gt[:, :, :], ALU.mult))
                link(v_.tensor_reduce(w_sum[:, :], ms[:, :, :], AX_X, ALU.add))
                link(v_.tensor_scalar(w_sum[:, :], w_sum[:, :], 1e-20, None, ALU.add))
                link(v_.reciprocal(w_sum[:, :], w_sum[:, :]))
                v_.scalar_tensor_tensor(comb[:, :, :], ms[:, :, :], ROUTE_SCALE,
                                        w_sum[:, :].unsqueeze(2).broadcast_to([P, NT, E]),
                                        ALU.mult, ALU.mult).then_inc(s_cb, 1)
                for c in range(NC):
                    dve.wait_ge(s_ct_hi, i * NC + c + 1)
                    cols = slice(512 * c, 512 * c + 512)
                    split_low(cT[32:32 + E, cols], PS[0:E, 6 + c, :], cT[0:E, cols]).then_inc(s_ct, 1)

                def add_residual(c):
                    dve.wait_ge(s_fo, i * NC + c + 1)
                    v_.tensor_tensor(H2[:, 4 * c:4 * c + 4, :], PS[:, 7, :].rearrange("p (n c) -> p n c", n=4),
                                     H2[:, 4 * c:4 * c + 4, :], ALU.add).then_inc(s_out, 1)

                for k in range(NK):
                    c, j = divmod(k, NJ)
                    routed = j < NJ - 1
                    dve.wait_ge(s_si, i * NK + k + 1)
                    dve.wait_ge(s_u, i * NK + k + 1)
                    if k >= 2:
                        dve.wait_ge(s_hc, i * NK + k - 1)
                    if routed:
                        v_.tensor_tensor(sg[:, k % 2, :], sg[:, k % 2, :], PS[:, 2 + k % 2, :],
                                         ALU.mult).then_inc(s_h1, 1)
                        n = c * (NJ - 1) + j
                        dve.wait_ge(s_h1, i * NK + k + 1)
                        dve.wait_ge(s_c, i * NCB + n + 1)
                        v_.tensor_tensor(hh[:, k % 2, :], sg[:, k % 2, :], PS[:, 4 + n % 2, :],
                                         ALU.mult).then_inc(s_h, 1)
                    else:
                        v_.tensor_tensor(hh[:, k % 2, :], sg[:, k % 2, :], PS[:, 2 + k % 2, :],
                                         ALU.mult).then_inc(s_h1, 1)
                        dve.wait_ge(s_h1, i * NK + k + 1)
                    if k == NJ + 2:
                        add_residual(0)
                add_residual(NC - 1)
                assert links[0] == DVE_LINKS, links[0]

        @block.tensor
        def _(pe):
            mm = nc.tensor.matmul

            def exact3(dst, l_hi, l_lo, r_hi, r_lo, start=True, **kw):
                mm(dst, l_hi, r_hi, start=start, stop=False, **kw)
                mm(dst, l_lo, r_hi, start=False, stop=False, **kw)
                return mm(dst, l_hi, r_lo, start=False, stop=True, **kw)

            pe.wait_ge(s_cst, 2)

            with pe.Fori(0, NG) as i:
                def transpose_in(ln):
                    for n in range(NT):
                        pe.wait_ge(s_xn, i * 2 * NT + ln * NT + n + 1)
                        ins = nc.tensor.transpose(PS[:, n // 4, P * (n % 4):P * (n % 4) + P], xn[:, n, :], ident)
                        if n % 4 == 3:
                            ins.then_inc(s_xt_ps, 1)

                transpose_in(0)
                for c in range(NC):
                    cols = slice(512 * c, 512 * c + 512)
                    pe.wait_ge(s_xt_lo, i * 2 * NC + c + 1)
                    exact3(PS[:, 2 + c, :], weight(w_hi, WQ), weight(w_lo, WQ), xT_hi[:, cols],
                           xT_lo[:, cols]).then_inc(s_q_ps, 1)
                    exact3(PS[:, 4 + c, :], weight(w_hi, WK), weight(w_lo, WK), xT_hi[:, cols],
                           xT_lo[:, cols]).then_inc(s_k_ps, 1)
                for n in range(NT):
                    r = slice(P * n, P * n + P)
                    ins = exact3(PS[:, 6 + n // 4, P * (n % 4):P * (n % 4) + P], xT_hi[:, r], xT_lo[:, r],
                                 weight(w_hi, WV), weight(w_lo, WV))
                    if n % 4 == 3:
                        ins.then_inc(s_vt_ps, 1)
                for n in range(2 * GB):
                    c, a = divmod(n, 4)
                    pe.wait_ge(s_v_lo, i * NC + (NC if a >= 2 else c + 1))
                    if n >= 4:
                        pe.wait_ge(s_v, i * 2 * GB + n - 3)
                    bank = (0, 1, 6, 7)[a]
                    mm(PS[:, bank, :], spreadq[:, a, :], v_hi[:, 4 * c:4 * c + 4, :], start=True, stop=False)
                    mm(PS[:, bank, :], spreadq[:, a, :], v_lo[:, 4 * c:4 * c + 4, :], start=False,
                       stop=True).then_inc(s_v_ps, 1)
                pe.wait_ge(s_q_lo, i * NC + NC)
                pe.wait_ge(s_k_lo, i * NC + NC)
                pe.wait_ge(s_v, i * 2 * GB + 2 * GB)

                for s in range(LAST_STEP):
                    if 0 <= s - 2 < NU:
                        u = s - 2
                        pe.wait_ge(s_mt, i * NU + u + 1)
                        j0 = Q if u % 4 == 0 else 0
                        for a in range(2):
                            dst = PS[:, 2 * (u % 2) + a, 0:4 * KW].rearrange("p (r k) -> p r k", r=4)
                            ins = mm(dst[:, :, j0:KW], mT[:, :], unit[:, 4 * a:4 * a + 4, j0:KW],
                                     start=False, stop=True, skip_group_check=True)
                        ins.then_inc(s_sm, 1)
                    if 0 <= s - 4 < NU:
                        b, p = divmod(s - 4, 4)
                        if p == 0:
                            if b >= 2:
                                pe.wait_ge(s_o, i * GB + b - 1)
                            mm(PS[:, 5 + b % 2, :], zero_bf[:, 0:P], zero_bf[:, :], start=True, stop=False,
                               skip_group_check=True)
                        pe.wait_ge(s_pt, i * NU + 4 * b + min(p + 1, 3) + 1)
                        for kb in (2 * p, 2 * p + 1):
                            nq = min(3, NQ - kb)
                            for g in range(HG):
                                pt = probsT[:, b % 2, g, :, :, :].rearrange("p t c q -> p (t c) q")
                                r0, c0 = 64 * (g % 2), T * (g // 2) + Q * kb
                                ins = mm(PS[r0:r0 + 64, 5 + b % 2, c0:c0 + Q * nq],
                                         v_bd[:, b * NQ + kb, g, :, :].rearrange("p k f -> p (k f)"),
                                         pt[:, 3 * kb + 2:3 * kb + 2 + 2 * nq - 1:2, :],
                                         start=False, stop=(kb == NQ - 1), skip_group_check=True)
                        if p == 3:
                            ins.then_inc(s_o_ps, 1)
                    if 0 <= s - 1 < NU:
                        u = s - 1
                        pe.wait_ge(s_m, i * NU + u + 1)
                        nc.tensor.transpose(PS[0:8, 4, 0:P], neg_max[:, u % 2, :], ident).then_inc(s_mt_ps, 1)
                    if s < NU:
                        b = s // 4
                        if s >= 2:
                            pe.wait_ge(s_p, i * NU + s - 1)
                        j0 = Q if s % 4 == 0 else 0
                        for a in range(2):
                            rows = slice(64 * a, 64 * a + 64)
                            dst = PS[:, 2 * (s % 2) + a, 0:4 * KW].rearrange("p (t e k) -> p t e k", t=2, e=2)
                            mm(dst[:, :, :, j0:KW].rearrange("p t e k -> p (t e) k"), ident4[rows, :],
                               band[rows, j0:KW].unsqueeze(1).broadcast_to([64, 4, KW - j0]),
                               start=True, stop=False, skip_group_check=True)
                        for tt in range(2):
                            t = 2 * (s % 4) + tt
                            nk = min(KW, (t + 1) * Q)
                            q1 = b * T + (t + 1) * Q
                            for l, z in ((q_hi, k_hi), (q_lo, k_hi), (q_hi, k_lo)):
                                for e in range(2):
                                    for a in range(2):
                                        rows = slice(64 * a, 64 * a + 64)
                                        dst = PS[:, 2 * (s % 2) + a, 0:4 * KW].rearrange("p (t e k) -> p t e k", t=2, e=2)
                                        ins = mm(dst[:, tt, e, KW - nk:KW],
                                                 l[rows, q1 // Q - 1, :, :].rearrange("p v q -> p (v q)"),
                                                 z[rows, e, q1 - nk:q1], start=False, stop=False,
                                                 skip_group_check=True)
                        ins.then_inc(s_s, 1)
                    b, at = divmod(s - 8, 4)
                    if 0 <= b < GB and at == 1:
                        pe.wait_ge(s_o, i * GB + b + 1)
                        if b >= 1:
                            pe.wait_ge(s_h2, i * NT + 2 * b)
                        for half in range(2):
                            for j in range(2):
                                n = 2 * half + j
                                ins = nc.tensor.transpose(PS[:, 7, P * n:P * n + P],
                                                          o_f[:, j, P * half:P * half + P], ident)
                        ins.then_inc(s_ot_ps, 1)
                    if 0 <= b < GB and at == 2:
                        pe.wait_ge(s_on, i * GB + b + 1)
                        for half in range(2):
                            ins = nc.tensor.transpose(PS[:, 7, P * half:P * half + P], o_n[:, half, :], ident)
                        ins.then_inc(s_ont_ps, 1)
                    if 0 <= b < GB and at == 3:
                        pe.wait_ge(s_ont, i * GB + b + 1)
                        for half in range(2):
                            r = slice(P * half, P * half + P)
                            ins = exact3(PS[:, 7, T + P * half:T + P * half + P], oT_hi[:, r], oT_lo[:, r],
                                         weight(w_hi, WO), weight(w_lo, WO))
                        ins.then_inc(s_y_ps, 1)

                transpose_in(1)
                pe.wait_ge(s_h2, i * NT + NT)
                for n in range(NT):
                    if n % 4 == 0:
                        pe.wait_ge(s_xt_lo, i * 2 * NC + NC + n // 4 + 1)
                    r = slice(P * n, P * n + P)
                    ins = exact3(PS[:, 7, E * n:E * n + E], xT_hi[:, r], xT_lo[:, r],
                                 weight(w_hi, GK, E), weight(w_lo, GK, E))
                ins.then_inc(s_lg, 1)

                def gate_up(k):
                    c, j = divmod(k, NJ)
                    cols = slice(512 * c, 512 * c + 512)
                    if k >= 2:
                        pe.wait_ge(s_si, i * NK + k - 1)
                    exact3(PS[:, k % 2, :], weight(w_hi, WG + P * j, P), weight(w_lo, WG + P * j, P),
                           xT_hi[:, cols], xT_lo[:, cols]).then_inc(s_g, 1)
                    if k >= 2:
                        pe.wait_ge(s_h1, i * NK + k - 1)
                    exact3(PS[:, 2 + k % 2, :], weight(w_hi, WU + P * j, P), weight(w_lo, WU + P * j, P),
                           xT_hi[:, cols], xT_lo[:, cols]).then_inc(s_u, 1)

                def spread(k):
                    c, j = divmod(k, NJ)
                    if j == NJ - 1:
                        return
                    n = c * (NJ - 1) + j
                    pe.wait_ge(s_ct, i * NC + c + 1)
                    if n >= 2:
                        pe.wait_ge(s_h, i * NCB + n - 1)
                    mm(PS[:, 4 + n % 2, :], pick[:, j, :], cT[:, 512 * c:512 * c + 512],
                       start=True, stop=True).then_inc(s_c, 1)

                def down(k):
                    c, j = divmod(k, NJ)
                    hidden_done(pe, i, k)
                    if j == 0 and c > 0:
                        pe.wait_ge(s_f, i * NC + c)
                    ins = mm(PS[:, 6, :], wd[:, j, :], hh[:, k % 2, :], start=(j == 0), stop=(j == NJ - 1))
                    ins.then_inc(s_hc, 1)

                def to_tokens(c):
                    pe.wait_ge(s_f, i * NC + c + 1)
                    if c > 0:
                        pe.wait_ge(s_out, i * NC + c)
                    for n in range(4):
                        ins = nc.tensor.transpose(PS[:, 7, P * n:P * n + P], y_f[:, P * n:P * n + P], ident)
                    ins.then_inc(s_fo, 1)

                gate_up(0)
                pe.wait_ge(s_cb, i + 1)
                for n in range(NT):
                    ins = nc.tensor.transpose(PS[0:E, 6 + n // 4, P * (n % 4):P * (n % 4) + P], comb[:, n, :], ident)
                    if n % 4 == 3:
                        ins.then_inc(s_ct_ps, 1)
                pe.wait_ge(s_ct, i * NC + NC)
                spread(0)
                for k in range(1, NK + 1):
                    if k < NK:
                        gate_up(k)
                        spread(k)
                    down(k - 1)
                    if k == NJ + 1:
                        to_tokens(0)
                to_tokens(NC - 1)


def kernel(**inputs):
    import numpy as np
    import concourse.bacc as _bacc
    from concourse import mybir as _mybir
    from concourse.bass_utils import run_bass_kernel_spmd as _run

    a = {k[3:]: np.asarray(v) for k, v in inputs.items()}
    both = [np.concatenate([a[f"ffn_w_{n}"].transpose(1, 0, 2).reshape(C, E * M), a[f"ffn_sw_{n}"]], axis=1)
            for n in ("gate", "up")]
    lanes = np.arange(P)

    cst = np.zeros((P, CONST_COLS), np.float32)

    def put(name, value):
        cst[:value.shape[0], CONST_AT[name]:CONST_AT[name] + CONSTS[name]] = value.reshape(value.shape[0], -1)

    put("ident", np.eye(P))
    put("headrow", (lanes[:, None] // D) % 4 == np.arange(4))
    put("grouprow", (lanes[:, None] // 32) % 2 == np.arange(2))
    put("headcol", lanes[:, None] // 32 == np.arange(32) // D)
    unit = np.repeat(np.eye(32)[:, :8, None], KW, axis=2)
    put("unit", np.concatenate([unit, unit]))
    pick = np.repeat(np.eye(32)[:, :E], M, axis=1)
    put("pick", np.concatenate([pick, pick]))
    i, j = np.arange(Q)[:, None], np.arange(KW)
    rows = np.zeros((P, 1)) + (lanes[:, None] % 64 < Q)
    put("band", rows * np.tile(np.where((j > i) & (j <= i + W), 0.0, -1e30), (4, 1)))
    put("spreadq", (lanes[:, None, None] == np.arange(4)[:, None] * 32 + lanes % 32))
    put("ident4", rows * np.tile(np.eye(Q), (4, 4)))
    put("lower", np.tile((np.arange(N_GROUP)[None, :] < np.arange(N_GROUP)[:, None]).reshape(1, -1), (P, 1)))

    arrays = {
        "x": a["attn_x"].reshape(B * T, C),
        "wq": a["attn_Wq"].T, "wk": a["attn_Wk"].T, "wv": a["attn_Wv"].T, "wo": a["attn_Wo"].T,
        "gate_w": a["ffn_gate_kernel"], "gate_b": a["ffn_gate_bias"],
        "w_gu": np.concatenate(both, axis=1),
        "w_down": a["ffn_w_down"].reshape(E * M, C), "sw_down": a["ffn_sw_down"],
        "consts": cst,
    }
    arrays = {k: np.ascontiguousarray(v) for k, v in arrays.items()}
    nc = _bacc.Bacc("TRN2", target_bir_lowering=False, num_devices=1)
    args = [nc.dram_tensor(k, v.shape, _mybir.dt.from_np(v.dtype), kind="ExternalInput").ap() for k, v in arrays.items()]
    out = nc.dram_tensor("out", (B * T, C), _mybir.dt.float32, kind="ExternalOutput").ap()
    preln_block_kernel(nc, *args, out)
    r = _run(nc, [arrays], core_ids=[0])
    return r.results[0]["out"].reshape(B, T, C)
```

```python
from collections import namedtuple
from contextlib import ExitStack

import concourse.bass as bass
from concourse import mybir

F32 = mybir.dt.float32
F32R = mybir.dt.float32r
BF16 = mybir.dt.bfloat16
ALU = mybir.AluOpType
ACT = mybir.ActivationFunctionType
AX_X = mybir.AxisListType.X

P = 128
B, T, C = 32, 256, 128
H, D, W = 16, 8, 64
E, M = 16, 64
TOP_K, N_GROUP, TOPK_GROUP, ROUTE_SCALE = 4, 4, 2, 2.5
EPS = 1e-5

GB = 2
NG = B // GB
TOK = GB * T
NT = TOK // P
Q = 32
NQ = T // Q
NSB = GB * NQ
HG = H // 4
KW = W + Q
NU = NSB // 2
NP = E // 2
NF = NP + 1
assert NU == NP == 8
STEPS = 8

LN1 = 0
XT = 1
QP, VP, RP = 2, 3, 4
QC = (4, 8)
KP = (6, 8)
SC = 8
PR = 9
PV = 11
OE = 14
OT, ON, OW = 15, 16, 17
LN2 = 18
XT2 = 19
LG = 24
CT = 26
SH = 26
FF = 27
DN = 28
YE = 35
YT = 38

BANK_A = 6
A_EARLY, A_SPREAD, A_LATE = range(3)
KEY_PLACE = (A_EARLY, A_LATE)
USES_A = sorted([(0, A_EARLY, LG), (1, A_EARLY, XT), (2, A_EARLY, QP), (3, A_EARLY, VP), (4, A_EARLY, RP),
                 (4, A_LATE, RP), (5, A_EARLY, RP + 1), (5, A_LATE, RP + 1), (6, A_EARLY, KP[0]), (6, A_LATE, YT), (0, A_LATE, KP[1]),
                 (3, A_LATE, XT2), (7, A_LATE, XT2 + 4)]
                + [((FF + k) % STEPS, A_SPREAD, FF + k) for k in range(NP)])
BANK_B = 3
B_POST, B_MAX = range(2)
USES_B = sorted([((st + 4 * b) % STEPS, B_POST, st + 4 * b) for st in (OT, ON, OW) for b in range(GB)]
                + [(CT % STEPS, B_POST, CT)] + [((SC + u) % STEPS, B_MAX, SC + u) for u in range(NU)])

LOOP_FIRST, LOOP_END = 6, NG
LAST_SLOT = NG - 1 + YT // STEPS

Slot = namedtuple("Slot", "n par fixed")
Group = namedtuple("Group", "n par fixed")


def at(slot, s, stage, stride=1, count=1):
    for k in range(count):
        d = stage + k * stride
        if d % STEPS == s:
            off = d // STEPS
            if slot.fixed and not 0 <= slot.n - off < NG:
                return None, 0
            return Group(slot.n - off, (slot.par + off) % 2, slot.fixed), k
    return None, 0


def uses_before(uses, slot, s, place):
    here = sum((a, b) < (s, place) for a, b, _ in uses)
    if not slot.fixed:
        return uses_before(uses, Slot(LOOP_FIRST, 0, True), 0, 0) + (slot.n - LOOP_FIRST) * len(uses) + here
    count = 0
    for n in range(slot.n + 1):
        for a, b, stage in uses:
            count += (n < slot.n or (a, b) < (s, place)) and 0 <= n - stage // STEPS < NG
    return count


def turn(g):
    return (g.n - g.par) * 8 + 16


CONSTS = {"ident": P, "headrow": 4, "grouprow": HG, "headcol": 32, "lower": N_GROUP * N_GROUP,
          "unit": 8 * KW, "pick": NP * P, "band": 2 * KW, "ident4": P, "spreadq": 4 * P}
CONST_AT, CONST_COLS = {}, 0
for _name, _cols in CONSTS.items():
    CONST_AT[_name] = CONST_COLS
    CONST_COLS += _cols
KEPT = CONST_AT["unit"]
WQ, WK, WV, WO, GK = 0, C, 2 * C, 3 * C, 4 * C
WG = GK + E
WU = WG + NF * P
W_COLS = WU + NF * P
LOADS = 11
ORDER_PER_SLOT = 29


def preln_block_kernel(nc, x, wq, wk, wv, wo, gate_w, gate_b, w_gu, w_down, sw_down, consts, out):
    with ExitStack() as ctx:
        def sb(name, shape, dt=F32):
            return ctx.enter_context(nc.sbuf_tensor(name, shape, dt))

        def sem(name):
            return ctx.enter_context(nc.semaphore(name))

        cst = sb("cst", [P, KEPT])
        w_hi = sb("w_hi", [P, W_COLS], F32R)
        w_lo = sb("w_lo", [P, W_COLS], F32R)
        wd = sb("wd", [P, NF, C])
        unit = sb("unit", [P, 8, KW], F32R)
        pick = sb("pick", [P, NP, P], F32R)
        band = sb("band", [P, 2, KW], BF16)
        ident4 = sb("ident4", [P, P], BF16)
        spreadq = sb("spreadq", [P, 4, P], F32R)
        zero_bf = sb("zero_bf", [1, 512], BF16)
        bias_b = sb("bias_b", [P, E])
        holder = sb("holder", [P, 1])
        X = sb("X", [P, 2, NT, C])
        X2 = sb("X2", [P, 2, NT, C])
        st1 = sb("st1", [P, NT, 6])
        mv1 = sb("mv1", [P, NT, 2])
        ve1 = sb("ve1", [P, NT])
        rs1 = sb("rs1", [P, NT])
        st2 = sb("st2", [P, 2, 6])
        mv2 = sb("mv2", [P, 2, 2])
        ve2 = sb("ve2", [P, 2])
        rs2 = sb("rs2", [P, 2])
        half_neg = sb("half_neg", [P, NT])
        eps = sb("eps", [P, NT])
        xn1 = sb("xn1", [P, NT, C])
        xT_hi = sb("xT_hi", [P, TOK], F32R)
        xT_lo = sb("xT_lo", [P, TOK], F32R)
        qr_hi = sb("qr_hi", [P, TOK], F32R)
        qr_lo = sb("qr_lo", [P, TOK], F32R)
        q_hi = sb("q_hi", [P, NSB, 4, Q], F32R)
        q_lo = sb("q_lo", [P, NSB, 4, Q], F32R)
        k_hi = sb("k_hi", [P, HG, TOK], F32R)
        k_lo = sb("k_lo", [P, HG, TOK], F32R)
        v_hi = sb("v_hi", [P, NT, C], F32R)
        v_lo = sb("v_lo", [P, NT, C], F32R)
        v_bd = sb("v_bd", [P, 2, NSB, HG, 2, 32])
        neg_max = sb("neg_max", [P, 8])
        mT = sb("mT", [P, P], F32R)
        probs = sb("probs", [P, 2, HG, KW])
        probsT = sb("probsT", [P, 2, HG, NQ, 3, Q])
        o_f = sb("o_f", [P, 2, T])
        o_rs = sb("o_rs", [P, 8, 4])
        o_n = sb("o_n", [P, 2, P])
        oT_hi = sb("oT_hi", [P, T], F32R)
        oT_lo = sb("oT_lo", [P, T], F32R)
        H2 = sb("H2", [P, 2, NT, C])
        OUT = sb("OUT", [P, 2, NT, C])
        xn2 = sb("xn2", [P, 2, C])
        x2_hi = sb("x2_hi", [P, 2, TOK], F32R)
        x2_lo = sb("x2_lo", [P, 2, TOK], F32R)
        th_r = sb("th_r", [P, NT * E])
        sc = sb("sc", [P, NT * E])
        pair = sb("pair", [P, NT * N_GROUP, 6])
        gs = sb("gs", [P, NT * N_GROUP])
        g_gt = sb("g_gt", [P, NT, N_GROUP, N_GROUP])
        g_eq = sb("g_eq", [P, NT, N_GROUP, N_GROUP])
        g_rank = sb("g_rank", [P, NT * N_GROUP])
        ms = sb("ms", [P, NT, E])
        m8 = sb("m8", [P, NT, 8])
        e_gt = sb("e_gt", [P, NT, E])
        e_eq = sb("e_eq", [P, NT, E])
        cum = sb("cum", [P, 2, NT, 8 + E])
        n_gt = sb("n_gt", [P, NT])
        w_sum = sb("w_sum", [P, NT])
        comb = sb("comb", [P, NT, E])
        cT = sb("cT", [P, 2, TOK], F32R)
        th = sb("th", [P, TOK])
        fa = sb("fa", [P, TOK])
        fb = sb("fb", [P, 2, TOK])
        spread = sb("spread", [P, 2, TOK])
        hh = sb("hh", [P, 2, TOK])
        hs = sb("hs", [P, TOK])
        y_f = sb("y_f", [P, TOK])
        spare = probsT[:, :, :, :, :, :].rearrange("p b g t c q -> p (b g t c q)")
        stage = spare[:, 0:W_COLS]
        cst_stage = spare[:, W_COLS:W_COLS + CONST_COLS - KEPT]

        PS = ctx.enter_context(nc.psum_tensor("PS", [P, 8, 512], F32))
        bank_a = PS[:, BANK_A, :]
        bank_b = PS[:, BANK_B, :]

        def const(name, rows=P):
            at_ = CONST_AT[name]
            if at_ >= KEPT:
                return cst_stage[0:rows, at_ - KEPT:at_ - KEPT + CONSTS[name]]
            return cst[0:rows, at_:at_ + CONSTS[name]]

        ident = const("ident")
        headrow = const("headrow")
        grouprow = const("grouprow")
        headcol = const("headcol")
        lower = const("lower").rearrange("p (i j) -> p i j", i=N_GROUP)

        def tiles(ap):
            return ap.rearrange("p (n c) -> p n c", c=C)

        def blocks(ap):
            return ap.rearrange("p (a q) -> p a q", q=Q)

        s_w = sem("weights_loaded")
        s_cst = sem("constants_ready")
        s_x = [sem("x_even_loaded"), sem("x_odd_loaded")]
        s_x2 = [sem("x_again_even_loaded"), sem("x_again_odd_loaded")]
        s_cp = [sem("h2_even_copied"), sem("h2_odd_copied")]
        s_st = [sem("even_stored"), sem("odd_stored")]
        s_mv1 = sem("mean_var1_ready")
        s_mv2 = sem("mean_var2_ready")
        s_rs1 = sem("rstd1_ready")
        s_rs2 = sem("rstd2_ready")
        s_pool = sem("pool_order")
        s_dve = sem("dve_order")
        s_xn1 = sem("xn1_ready")
        s_xn2 = sem("xn2_ready")
        s_a_ps = sem("bank_a_filled")
        s_a_hi = sem("bank_a_high")
        s_a = sem("bank_a_taken")
        s_b_ps = sem("bank_b_filled")
        s_b_hi = sem("bank_b_high")
        s_b = sem("bank_b_taken")
        s_q = sem("q_copies_ready")
        s_s = sem("scores_ready")
        s_m = sem("neg_max_ready")
        s_sm = sem("scores_less_max")
        s_p = sem("probs_ready")
        s_pt = sem("probsT_ready")
        s_o_ps = sem("o_in_psum")
        s_o = sem("o_ready")
        s_on = sem("o_norm_ready")
        s_cb = sem("combine_ready")
        s_g = sem("gate_in_psum")
        s_u = sem("up_in_psum")
        s_th = sem("tanh_ready")
        s_fa = sem("silu2_ready")
        s_fb = sem("silu2_up_ready")
        s_h = sem("hidden_ready")
        s_dn = sem("ffn_in_psum")
        s_y = sem("ffn_ready")

        def a_before(slot, s, place):
            return uses_before(USES_A, slot, s, place)

        def b_before(slot, s, place):
            return uses_before(USES_B, slot, s, place)

        x_t = x.rearrange("(g n p) c -> g p n c", n=NT, p=P)
        out_t = out.rearrange("(g n p) c -> g p n c", n=NT, p=P)

        def run_slots(eng, body):
            for n in range(LOOP_FIRST):
                body(Slot(n, n % 2, True))
            with eng.Fori(LOOP_FIRST // 2, LOOP_END // 2) as pair_of_slots:
                body(Slot(pair_of_slots * 2, 0, False))
                body(Slot(pair_of_slots * 2 + 1, 1, False))
            for n in range(LOOP_END, LAST_SLOT + 1):
                body(Slot(n, n % 2, True))

        block = ctx.enter_context(nc.Block())

        @block.sync
        def _(sp):
            sp.dma_start(X[:, 0, :, :], x_t[0]).then_inc(s_x[0], 16)
            sp.dma_start(cst[:, :], consts[:, 0:KEPT]).then_inc(s_w, 16)
            for n, w in ((WQ, wq), (WK, wk), (WV, wv), (WO, wo)):
                sp.dma_start(stage[:, n:n + C], w).then_inc(s_w, 16)
            sp.dma_start(stage[:, GK:GK + E], gate_w).then_inc(s_w, 16)
            sp.dma_start(stage[:, WG:W_COLS], w_gu).then_inc(s_w, 16)
            sp.dma_start(cst_stage, consts[:, KEPT:CONST_COLS]).then_inc(s_w, 16)
            sp.dma_start(wd[:, 0:NP, :], w_down.rearrange("(j p) c -> p j c", p=P)).then_inc(s_w, 16)
            sp.dma_start(wd[:, NP, :], sw_down).then_inc(s_w, 16)
            sp.dma_start(bias_b[:, :], gate_b.partition_broadcast(P)).then_inc(s_w, 16)

            def load_x(g):
                if not (g.fixed and g.n < 2):
                    sp.wait_ge(s_xn1, (g.n - 1) * NT)
                sp.dma_start(X[:, g.par, :, :], x_t[g.n]).then_inc(s_x[g.par], 16)

            def slot(sl):
                if not (sl.fixed and not 0 < sl.n < NG):
                    load_x(Group(sl.n, sl.par, sl.fixed))
                g, _ = at(sl, 25 % STEPS, 25)
                if g:
                    sp.wait_ge(s_b, b_before(sl, 0, 0))
                    if not (g.fixed and g.n < 2):
                        sp.wait_ge(s_st[g.par], turn(g) - 16)
                    sp.dma_start(OUT[:, g.par, :, :], H2[:, g.par, :, :]).then_inc(s_cp[g.par], 16)
                g, _ = at(sl, 12 % STEPS, 12)
                if g:
                    if not (g.fixed and g.n < 2):
                        sp.wait_ge(s_b, b_before(sl, (OW + 4) % STEPS, B_MAX))
                    sp.dma_start(X2[:, g.par, :, :], x_t[g.n]).then_inc(s_x2[g.par], 16)
                g, _ = at(sl, YT % STEPS, YT)
                if g:
                    sp.wait_ge(s_a, a_before(sl, YT % STEPS, A_LATE) + 1)
                    sp.dma_start(out_t[g.n], OUT[:, g.par, :, :]).then_inc(s_st[g.par], 16)

            run_slots(sp, slot)
            for par in range(2):
                sp.wait_ge(s_st[par], 16 * NG // 2)

        @block.gpsimd
        def _(pool):
            tt = nc.gpsimd.tensor_tensor
            nc.gpsimd.memset(half_neg[:, :], -0.5).then_inc(s_pool, 1)
            nc.gpsimd.memset(eps[:, :], EPS).then_inc(s_pool, 1)
            pool.wait_ge(s_pool, 2)
            pool.wait_ge(s_w, 16 * LOADS)

            def slot(sl):
                for s in range(STEPS):
                    g, _ = at(sl, s, LN1)
                    if g:
                        pool.wait_ge(s_mv1, g.n + 1)
                        tt(ve1[:, :], mv1[:, :, 1], eps[:, :], ALU.add).then_inc(s_rs1, 1)
                        pool.wait_ge(s_rs1, 2 * g.n + 1)
                        tt(rs1[:, :], ve1[:, :], half_neg[:, :], ALU.pow).then_inc(s_rs1, 1)
                    g, b = at(sl, s, LN2, 4, GB)
                    if g:
                        pool.wait_ge(s_mv2, g.n * GB + b + 1)
                        tt(ve2[:, :], mv2[:, :, 1], eps[:, 0:2], ALU.add).then_inc(s_rs2, 1)
                        pool.wait_ge(s_rs2, (g.n * GB + b) * 2 + 1)
                        tt(rs2[:, :], ve2[:, :], half_neg[:, 0:2], ALU.pow).then_inc(s_rs2, 1)
                    for b in range(GB):
                        g, pair_ = at(sl, s, QC[b], 1, 2)
                        if not g:
                            continue
                        if pair_ == 0:
                            if b == 0:
                                pool.wait_ge(s_a, a_before(sl, QP % STEPS, A_EARLY) + 1)
                            if not (g.fixed and g.n == 0):
                                pool.wait_ge(s_s, (g.n - 1) * NU + 4 * b + 4)
                        for a in (2 * pair_, 2 * pair_ + 1):
                            for src, dst in ((qr_hi, q_hi), (qr_lo, q_lo)):
                                tt(dst[:, NQ * b:NQ * b + NQ, a, :], blocks(src[:, T * b:T * b + T].bitcast(F32)),
                                   headrow[:, a:a + 1].unsqueeze(2).broadcast_to([P, NQ, Q]), ALU.mult).then_inc(s_q, 1)
                    g, k = at(sl, s, FF, 1, NP)
                    if g:
                        pool.wait_ge(s_fb, g.n * NF + k + 2)
                        pool.wait_ge(s_a, a_before(sl, s, A_SPREAD) + 1)
                        tt(hh[:, k % 2, :], fb[:, k % 2, :], spread[:, k % 2, :], ALU.mult).then_inc(s_h, 1)

            run_slots(pool, slot)

        @block.scalar
        def _(act):
            def copy(dst, src, **kw):
                return nc.scalar.activation(dst, src, ACT.Copy, **kw)

            act.wait_ge(s_w, 16 * LOADS)
            copy(w_hi[:, :], stage).then_inc(s_cst, 1)

            def slot(sl):
                for s in range(STEPS):
                    g, u = at(sl, s, PR, 1, NU)
                    if g:
                        act.wait_ge(s_sm, g.n * NU + u + 1)
                        j0 = Q if u % 4 == 0 else 0
                        src = PS[:, 0:2, 0:HG * KW].rearrange("p t (g k) -> p t g k", g=HG)
                        nc.scalar.activation(probs[:, :, :, j0:KW], src[:, :, :, j0:KW], ACT.Exp,
                                             scale=float(D) ** -0.5).then_inc(s_p, 1)

                    def filled(place):
                        act.wait_ge(s_a_ps, a_before(sl, s, place) + 1)

                    for stage_, dst in ((XT, xT_hi[:, :]), (QP, qr_hi[:, :])):
                        g, _ = at(sl, s, stage_)
                        if g:
                            if stage_ == QP and not (g.fixed and g.n == 0):
                                act.wait_ge(s_q, g.n * 16)
                            filled(A_EARLY)
                            copy(dst, bank_a).then_inc(s_a_hi, 1)
                    g, _ = at(sl, s, VP)
                    if g:
                        filled(A_EARLY)
                        copy(v_hi[:, :, :], tiles(bank_a)).then_inc(s_a_hi, 1)
                    def keys(b):
                        g, _ = at(sl, s, KP[b])
                        if g:
                            filled(KEY_PLACE[b])
                            for a in range(HG):
                                ins = copy(k_hi[:, a, T * b:T * b + T], bank_a[:, 0:T], scale=grouprow[:, a:a + 1])
                            ins.then_inc(s_a_hi, 1)

                    keys(0)
                    g, _ = at(sl, s, LG)
                    if g:
                        filled(A_EARLY)
                        nc.scalar.activation(th_r[:, :], bank_a[:, 0:NT * E], ACT.Tanh, scale=0.5).then_inc(s_a, 1)

                    g, k = at(sl, s, FF, 1, NP)
                    if g:
                        act.wait_ge(s_g, g.n * NF + k + 2)
                        nc.scalar.activation(th[:, :], PS[:, 4, :], ACT.Tanh, scale=0.5).then_inc(s_th, 1)
                        filled(A_SPREAD)
                        copy(spread[:, k % 2, :], bank_a).then_inc(s_a, 1)

                    g, b = at(sl, s, ON, 4, GB)
                    if g:
                        act.wait_ge(s_b_ps, b_before(sl, s, B_POST) + 1)
                        copy(oT_hi[:, :], bank_b[:, 0:T]).then_inc(s_b_hi, 1)
                    g, _ = at(sl, s, CT)
                    if g:
                        act.wait_ge(s_b_ps, b_before(sl, s, B_POST) + 1)
                        copy(cT[0:E, g.par, :], PS[0:E, BANK_B, :]).then_inc(s_b_hi, 1)
                    g, u = at(sl, s, SC, 1, NU)
                    if g:
                        act.wait_ge(s_b_ps, b_before(sl, s, B_MAX) + 1)
                        copy(mT[0:8, :], PS[0:8, BANK_B, 0:P]).then_inc(s_b_hi, 1)

                    g, b = at(sl, s, OE, 4, GB)
                    if g:
                        act.wait_ge(s_o_ps, g.n * GB + b + 1)
                        copy(o_f[:, :, :], PS[:, 2, :].rearrange("p (j q) -> p j q", j=2)).then_inc(s_o, 1)
                    g, _ = at(sl, s, SH)
                    if g:
                        act.wait_ge(s_g, g.n * NF + 1)
                        act.wait_ge(s_fa, g.n * NF)
                        nc.scalar.activation(th[:, :], PS[:, 4, :], ACT.Tanh, scale=0.5).then_inc(s_th, 1)
                    keys(1)
                    g, b = at(sl, s, XT2, 4, GB)
                    if g:
                        filled(A_LATE)
                        copy(x2_hi[:, g.par, T * b:T * b + T], bank_a[:, 0:T]).then_inc(s_a_hi, 1)
                    g, _ = at(sl, s, YE)
                    if g:
                        act.wait_ge(s_dn, g.n + 1)
                        copy(y_f[:, :], PS[:, 7, :]).then_inc(s_y, 1)

            run_slots(act, slot)

        @block.vector
        def _(dve):
            v_ = nc.vector
            v_.memset(zero_bf[:, :], 0.0)
            v_.memset(mT[:, :].bitcast(F32), 0.0)
            v_.memset(cT[:, :, :].bitcast(F32), 0.0)
            v_.memset(cum[:, :, :, :], 0.0)
            dve.wait_ge(s_w, 16 * LOADS)
            for n in range(2 * NSB):
                v_.tensor_copy(v_bd[:, n // NSB, n % NSB, :, 1, :], headcol.unsqueeze(1).broadcast_to([P, HG, 32]))
            v_.tensor_copy(spreadq[:, :, :], const("spreadq").rearrange("p (a k) -> p a k", a=4))
            v_.tensor_copy(unit[:, :, :], const("unit").rearrange("p (r k) -> p r k", r=8))
            v_.tensor_copy(pick[:, :, :], const("pick").rearrange("p (j k) -> p j k", k=P))
            v_.tensor_copy(band[:, :, :], const("band").rearrange("p (a k) -> p a k", a=2))
            v_.tensor_copy(ident4[:, :], const("ident4"))
            dve.wait_ge(s_cst, 1)
            v_.tensor_tensor(w_lo[:, :], stage, w_hi[:, :].bitcast(F32), ALU.subtract).then_inc(s_cst, 1)
            dve.wait_ge(s_cst, 2)

            order = {"before": 0, "done": 0}

            def link(sl, ins):
                order["done"] += 1
                ins.then_inc(s_dve, 1)
                loop = 0 if sl.fixed else (sl.n - LOOP_FIRST) * ORDER_PER_SLOT
                dve.wait_ge(s_dve, order["before"] + loop + order["done"])

            def split_low(dst, src, high):
                return v_.tensor_tensor(dst, src, high.bitcast(F32), ALU.subtract)

            def split_high_count(uses, split, sl, s, place):
                return uses_before([x for x in uses if split(x)], sl, s, place) + 1

            def a_high(sl, s, place):
                dve.wait_ge(s_a_hi, split_high_count(
                    USES_A, lambda x: x[2] in (XT, QP, VP, *KP, XT2, XT2 + 4), sl, s, place))

            def b_high(sl, s, place):
                dve.wait_ge(s_b_hi, split_high_count(
                    USES_B, lambda x: x[1] == B_MAX or x[2] in (ON, ON + 4, CT), sl, s, place))

            def stats(sl, src, n, st, mv):
                for a in range(n):
                    ins = v_.bn_stats(st[:, a, :], src[:, a, :])
                link(sl, ins)
                v_.memset(holder[:, :], 0.0)
                for a in range(n):
                    ins = v_.bn_aggr(mv[:, a, :], st[:, a, :])
                return ins

            def normalise(dst, src, n, mv, rs, done):
                for a in range(n):
                    v_.tensor_scalar(dst[:, a, :], src[:, a, :], mv[:, a, 0:1], rs[:, a:a + 1],
                                     ALU.subtract, ALU.mult).then_inc(done, 1)

            def routing_groups(sl):
                link(sl, v_.tensor_scalar(sc[:, :], th_r[:, :], 0.5, 0.5, ALU.mult, ALU.add))
                sc3 = sc[:, :].rearrange("p (n e) -> p n e", n=NT)
                link(sl, v_.tensor_tensor(sc3, sc3, bias_b[:, :].unsqueeze(1).broadcast_to([P, NT, E]), ALU.add))
                s4 = sc[:, :].rearrange("p (n e) -> p n e", e=4)
                v_.tensor_tensor(pair[:, :, 0:3], s4[:, :, 0:3], s4[:, :, 1:4], ALU.add)
                v_.tensor_tensor(pair[:, :, 3:5], s4[:, :, 0:2], s4[:, :, 2:4], ALU.add)
                link(sl, v_.tensor_tensor(pair[:, :, 5:6], s4[:, :, 0:1], s4[:, :, 3:4], ALU.add))
                link(sl, v_.tensor_reduce(gs[:, :], pair[:, :, :], AX_X, ALU.max))
                gs3 = gs[:, :].rearrange("p (n g) -> p n g", n=NT)
                g_j = gs3.unsqueeze(2).broadcast_to([P, NT, N_GROUP, N_GROUP])
                g_i = gs3.unsqueeze(3).broadcast_to([P, NT, N_GROUP, N_GROUP])
                v_.tensor_tensor(g_gt[:, :, :, :], g_j, g_i, ALU.is_gt)
                link(sl, v_.tensor_tensor(g_eq[:, :, :, :], g_j, g_i, ALU.is_equal))
                link(sl, v_.tensor_tensor(g_eq[:, :, :, :], g_eq[:, :, :, :],
                                          lower.unsqueeze(1).broadcast_to([P, NT, N_GROUP, N_GROUP]), ALU.mult))
                link(sl, v_.tensor_tensor(g_gt[:, :, :, :], g_gt[:, :, :, :], g_eq[:, :, :, :], ALU.add))
                link(sl, v_.tensor_reduce(g_rank[:, :], g_gt[:, :, :, :].rearrange("p n i j -> p (n i) j"),
                                          AX_X, ALU.add))
                link(sl, v_.tensor_scalar(g_rank[:, :], g_rank[:, :], float(TOPK_GROUP), None, ALU.is_lt))
                link(sl, v_.tensor_tensor(ms[:, :, :].rearrange("p n (g e) -> p (n g) e", g=N_GROUP), s4,
                                          g_rank[:, :].unsqueeze(2).broadcast_to([P, NT * N_GROUP, 4]), ALU.mult))

            def routing_experts(sl):
                v_.memset(holder[:, :], 0.0)
                for n in range(NT):
                    ins = v_.max(m8[:, n, :], ms[:, n, :])
                link(sl, ins)
                fourth = m8[:, :, TOP_K - 1:TOP_K].broadcast_to([P, NT, E])
                v_.tensor_tensor(e_gt[:, :, :], ms[:, :, :], fourth, ALU.is_gt)
                v_.tensor_tensor(e_eq[:, :, :], ms[:, :, :], fourth, ALU.is_equal)
                link(sl, v_.tensor_tensor(cum[:, 0, :, 8:8 + E], ms[:, :, :], fourth, ALU.is_equal))
                for n, d in enumerate((1, 2, 4, 8)):
                    a, z = n % 2, 1 - n % 2
                    link(sl, v_.tensor_tensor(cum[:, z, :, 8:8 + E], cum[:, a, :, 8:8 + E],
                                              cum[:, a, :, 8 - d:8 + E - d], ALU.add))
                link(sl, v_.tensor_reduce(n_gt[:, :], e_gt[:, :, :], AX_X, ALU.add))
                link(sl, v_.tensor_tensor(cum[:, 1, :, 8:8 + E], cum[:, 0, :, 8:8 + E],
                                          n_gt[:, :].unsqueeze(2).broadcast_to([P, NT, E]), ALU.add))
                link(sl, v_.scalar_tensor_tensor(e_eq[:, :, :], cum[:, 1, :, 8:8 + E], float(TOP_K), e_eq[:, :, :],
                                                 ALU.is_le, ALU.mult))
                link(sl, v_.tensor_tensor(e_gt[:, :, :], e_gt[:, :, :], e_eq[:, :, :], ALU.add))
                link(sl, v_.tensor_tensor(ms[:, :, :], ms[:, :, :], e_gt[:, :, :], ALU.mult))
                link(sl, v_.tensor_reduce(w_sum[:, :], ms[:, :, :], AX_X, ALU.add))
                link(sl, v_.tensor_scalar(w_sum[:, :], w_sum[:, :], 1e-20, None, ALU.add))
                link(sl, v_.reciprocal(w_sum[:, :], w_sum[:, :]))
                v_.scalar_tensor_tensor(comb[:, :, :], ms[:, :, :], ROUTE_SCALE,
                                        w_sum[:, :].unsqueeze(2).broadcast_to([P, NT, E]),
                                        ALU.mult, ALU.mult).then_inc(s_cb, 1)

            def slot(sl):
                order["done"] = 0 if sl.fixed or sl.par == 0 else order["done"]
                if not sl.fixed and sl.par == 1:
                    order["done"] = 0
                for s in range(STEPS):
                    g, u = at(sl, s, PR, 1, NU)
                    if g:
                        b, t0 = u // 4, 2 * (u % 4)
                        dve.wait_ge(s_p, g.n * NU + u + 1)
                        c0 = 1 if u % 4 == 0 else 0
                        for tt in range(2):
                            ins = v_.transpose(
                                probsT[:, b, :, t0 + tt, c0:3, :].rearrange("p g c q -> p g (c q)"),
                                probs[:, tt, :, c0 * Q:KW])
                        ins.then_inc(s_pt, 1)

                    for stage_, dst, high in ((XT, xT_lo, xT_hi), (QP, qr_lo, qr_hi)):
                        g, _ = at(sl, s, stage_)
                        if g:
                            if stage_ == QP and not (g.fixed and g.n == 0):
                                dve.wait_ge(s_q, g.n * 16)
                            a_high(sl, s, A_EARLY)
                            split_low(dst[:, :], bank_a, high[:, :]).then_inc(s_a, 1)
                    g, _ = at(sl, s, VP)
                    if g:
                        a_high(sl, s, A_EARLY)
                        split_low(v_lo[:, :, :], tiles(bank_a), v_hi[:, :, :]).then_inc(s_a, 1)
                    def keys(b):
                        g, _ = at(sl, s, KP[b])
                        if g:
                            a_high(sl, s, KEY_PLACE[b])
                            for a in range(HG):
                                r = slice(T * b, T * b + T)
                                ins = v_.scalar_tensor_tensor(k_lo[:, a, r], bank_a[:, 0:T], grouprow[:, a:a + 1],
                                                              k_hi[:, a, r].bitcast(F32), ALU.mult, ALU.subtract)
                            ins.then_inc(s_a, 1)

                    keys(0)

                    def values(place, a):
                        dve.wait_ge(s_a_ps, a_before(sl, s, place) + 1)
                        v_.tensor_tensor(v_bd[:, g.par, a:a + 13:4, :, 0, :],
                                         bank_a.rearrange("p (n g f) -> p n g f", g=HG, f=32),
                                         headcol.unsqueeze(1).unsqueeze(1).broadcast_to([P, NT, HG, 32]),
                                         ALU.mult).then_inc(s_a, 1)

                    g, half = at(sl, s, RP, 1, 2)
                    if g:
                        values(A_EARLY, 2 * half)

                    g, _ = at(sl, s, LN1)
                    if g:
                        dve.wait_ge(s_x[g.par], turn(g))
                        stats(sl, X[:, g.par, :, :], NT, st1, mv1).then_inc(s_mv1, 1)
                    g, b = at(sl, s, LN2, 4, GB)
                    if g:
                        dve.wait_ge(s_b, b_before(sl, s, 0))
                        stats(sl, H2[:, g.par, 2 * b:2 * b + 2, :], 2, st2, mv2).then_inc(s_mv2, 1)

                    g, k = at(sl, s, FF, 1, NP)
                    if g:
                        f = g.n * NF + k + 2
                        dve.wait_ge(s_th, f)
                        v_.scalar_tensor_tensor(fa[:, :], th[:, :], 1.0, PS[:, 4, :], ALU.add,
                                                ALU.mult).then_inc(s_fa, 1)
                        dve.wait_ge(s_fa, f)
                        dve.wait_ge(s_u, f)
                        v_.tensor_tensor(fb[:, k % 2, :], fa[:, :], PS[:, 5, :], ALU.mult).then_inc(s_fb, 1)

                    g, u = at(sl, s, SC, 1, NU)
                    if g:
                        dve.wait_ge(s_s, g.n * NU + u + 1)
                        j0 = Q if u % 4 == 0 else 0
                        src = PS[:, 0:2, 0:HG * KW].rearrange("p t (g k) -> p t g k", g=HG)
                        v_.tensor_reduce(neg_max[:, :].rearrange("p (t g) -> p t g", t=2), src[:, :, :, j0:KW],
                                         AX_X, ALU.max, negate=True).then_inc(s_m, 1)

                    g, b = at(sl, s, OT, 4, GB)
                    if g:
                        dve.wait_ge(s_b_ps, b_before(sl, s, B_POST) + 1)
                        o_t = bank_b.rearrange("p (a k v d) -> p a k v d", k=2, v=4, d=D)
                        link(sl, v_.reciprocal(o_rs[:, :, :], o_t[:, :, 1, :, 0]))
                        v_.tensor_tensor(o_n[:, :, :].rearrange("p n (a v d) -> p (n a) v d", v=4, d=D),
                                         o_t[:, :, 0, :, :],
                                         o_rs[:, :, :].unsqueeze(3).broadcast_to([P, 8, 4, D]),
                                         ALU.mult).then_inc(s_b, 1)
                    g, b = at(sl, s, ON, 4, GB)
                    if g:
                        b_high(sl, s, B_POST)
                        split_low(oT_lo[:, :], bank_b[:, 0:T], oT_hi[:, :]).then_inc(s_b, 1)
                    g, b = at(sl, s, OW, 4, GB)
                    if g:
                        dve.wait_ge(s_b_ps, b_before(sl, s, B_POST) + 1)
                        dve.wait_ge(s_x2[g.par], turn(g))
                        if b == 0 and not (g.fixed and g.n < 2):
                            dve.wait_ge(s_cp[g.par], turn(g) - 16)
                        v_.tensor_tensor(H2[:, g.par, 2 * b:2 * b + 2, :], tiles(bank_b[:, 0:T]),
                                         X2[:, g.par, 2 * b:2 * b + 2, :], ALU.add).then_inc(s_b, 1)
                    g, _ = at(sl, s, CT)
                    if g:
                        b_high(sl, s, B_POST)
                        split_low(cT[32:32 + E, g.par, :], PS[0:E, BANK_B, :], cT[0:E, g.par, :]).then_inc(s_b, 1)

                    g, u = at(sl, s, SC, 1, NU)
                    if g:
                        b_high(sl, s, B_MAX)
                        split_low(mT[32:40, :], PS[0:8, BANK_B, 0:P], mT[0:8, :]).then_inc(s_b, 1)

                    g, _ = at(sl, s, LN1)
                    if g:
                        dve.wait_ge(s_mv1, g.n + 1)
                        dve.wait_ge(s_rs1, 2 * g.n + 2)
                        normalise(xn1, X[:, g.par, :, :], NT, mv1, rs1, s_xn1)
                    g, b = at(sl, s, LN2, 4, GB)
                    if g:
                        dve.wait_ge(s_mv2, g.n * GB + b + 1)
                        dve.wait_ge(s_rs2, (g.n * GB + b) * 2 + 2)
                        normalise(xn2, H2[:, g.par, 2 * b:2 * b + 2, :], 2, mv2, rs2, s_xn2)

                    g, half = at(sl, s, RP, 1, 2)
                    if g:
                        values(A_LATE, 2 * half + 1)
                    keys(1)
                    g, b = at(sl, s, XT2, 4, GB)
                    if g:
                        a_high(sl, s, A_LATE)
                        cols = slice(T * b, T * b + T)
                        split_low(x2_lo[:, g.par, cols], bank_a[:, 0:T], x2_hi[:, g.par, cols]).then_inc(s_a, 1)
                    g, _ = at(sl, s, YT)
                    if g:
                        dve.wait_ge(s_a_ps, a_before(sl, s, A_LATE) + 1)
                        dve.wait_ge(s_cp[g.par], turn(g))
                        v_.tensor_tensor(OUT[:, g.par, :, :], tiles(bank_a), OUT[:, g.par, :, :],
                                         ALU.add).then_inc(s_a, 1)
                    g, _ = at(sl, s, LG)
                    if g:
                        dve.wait_ge(s_a, a_before(sl, s, A_EARLY) + 1)
                        routing_groups(sl)
                    g, _ = at(sl, s, LG + 1)
                    if g:
                        routing_experts(sl)
                    g, _ = at(sl, s, SH)
                    if g:
                        f = g.n * NF + 1
                        dve.wait_ge(s_th, f)
                        v_.scalar_tensor_tensor(fa[:, :], th[:, :], 1.0, PS[:, 4, :], ALU.add,
                                                ALU.mult).then_inc(s_fa, 1)
                        dve.wait_ge(s_fa, f)
                        dve.wait_ge(s_u, f)
                        v_.scalar_tensor_tensor(hs[:, :], fa[:, :], 0.5, PS[:, 5, :], ALU.mult,
                                                ALU.mult).then_inc(s_fb, 1)
                if sl.fixed:
                    order["before"] += order["done"]
                else:
                    assert order["done"] == ORDER_PER_SLOT, order["done"]
                    if sl.par == 1:
                        order["before"] += (LOOP_END - LOOP_FIRST) * ORDER_PER_SLOT

            run_slots(dve, slot)

        @block.tensor
        def _(pe):
            mm = nc.tensor.matmul

            def exact3(dst, l_hi, l_lo, r_hi, r_lo):
                mm(dst, l_hi, r_hi, start=True, stop=False)
                mm(dst, l_lo, r_hi, start=False, stop=False)
                return mm(dst, l_hi, r_lo, start=False, stop=True)

            def w2(n, cols=C):
                return w_hi[:, n:n + cols], w_lo[:, n:n + cols]

            pe.wait_ge(s_cst, 2)

            def gate_up(g, j, f):
                if not (g.fixed and g.n == 0 and f == 0):
                    pe.wait_ge(s_fb, g.n * NF + f)
                x2 = x2_hi[:, g.par, :], x2_lo[:, g.par, :]
                exact3(PS[:, 4, :], *w2(WG + P * j), *x2).then_inc(s_g, 1)
                exact3(PS[:, 5, :], *w2(WU + P * j), *x2).then_inc(s_u, 1)

            def slot(sl):
                for s in range(STEPS):
                    g, u = at(sl, s, PR, 1, NU)
                    if g:
                        pe.wait_ge(s_b, b_before(sl, s, 0))
                        j0 = Q if u % 4 == 0 else 0
                        for tt in range(2):
                            dst = PS[:, tt, 0:HG * KW].rearrange("p (g k) -> p g k", g=HG)
                            ins = mm(dst[:, :, j0:KW], mT[:, :], unit[:, HG * tt:HG * tt + HG, j0:KW],
                                     start=False, stop=True, skip_group_check=True)
                        ins.then_inc(s_sm, 1)

                    def bank_a_free(place):
                        if not (sl.fixed and a_before(sl, s, place) == 0):
                            pe.wait_ge(s_a, a_before(sl, s, place))

                    g, _ = at(sl, s, XT)
                    if g:
                        bank_a_free(A_EARLY)
                        pe.wait_ge(s_xn1, g.n * NT + NT)
                        for n in range(NT):
                            ins = nc.tensor.transpose(bank_a[:, P * n:P * n + P], xn1[:, n, :], ident)
                        ins.then_inc(s_a_ps, 1)
                    g, _ = at(sl, s, QP)
                    if g:
                        bank_a_free(A_EARLY)
                        exact3(bank_a, *w2(WQ), xT_hi[:, :], xT_lo[:, :]).then_inc(s_a_ps, 1)

                    def keys(b):
                        g, _ = at(sl, s, KP[b])
                        if g:
                            bank_a_free(KEY_PLACE[b])
                            r = slice(T * b, T * b + T)
                            exact3(bank_a[:, 0:T], *w2(WK), xT_hi[:, r], xT_lo[:, r]).then_inc(s_a_ps, 1)

                    keys(0)
                    g, _ = at(sl, s, VP)
                    if g:
                        bank_a_free(A_EARLY)
                        for n in range(NT):
                            r = slice(P * n, P * n + P)
                            ins = exact3(bank_a[:, r], xT_hi[:, r], xT_lo[:, r], *w2(WV))
                        ins.then_inc(s_a_ps, 1)

                    def values(place, a):
                        bank_a_free(place)
                        mm(bank_a, spreadq[:, a, :], v_hi[:, :, :], start=True, stop=False)
                        mm(bank_a, spreadq[:, a, :], v_lo[:, :, :], start=False, stop=True).then_inc(s_a_ps, 1)

                    g, half = at(sl, s, RP, 1, 2)
                    if g:
                        values(A_EARLY, 2 * half)
                    g, _ = at(sl, s, LG)
                    if g:
                        bank_a_free(A_EARLY)
                        for n in range(NT):
                            r = slice(P * n, P * n + P)
                            ins = exact3(bank_a[:, E * n:E * n + E], x2_hi[:, g.par, r], x2_lo[:, g.par, r],
                                         *w2(GK, E))
                        ins.then_inc(s_a_ps, 1)

                    g, k = at(sl, s, FF, 1, NP)
                    if g:
                        gate_up(g, k, k + 1)

                    g, u = at(sl, s, SC, 1, NU)
                    if g:
                        if u == 0:
                            pe.wait_ge(s_q, g.n * 16 + 8)
                            pe.wait_ge(s_a, a_before(Slot(sl.n - 1, 1 - sl.par, sl.fixed), KP[0], A_EARLY) + 1)
                        if u == NU // 2:
                            pe.wait_ge(s_q, g.n * 16 + 16)
                            pe.wait_ge(s_a, a_before(sl, KP[1] % STEPS, A_LATE) + 1)
                        if not (g.fixed and g.n == 0 and u == 0):
                            pe.wait_ge(s_p, g.n * NU + u)
                        j0 = Q if u % 4 == 0 else 0
                        for tt in range(2):
                            t = 2 * (u % 4) + tt
                            dst = PS[:, tt, 0:HG * KW].rearrange("p (g k) -> p g k", g=HG)
                            mm(dst[:, :, j0:KW], ident4[:, :],
                               band[:, int(t == 0), j0:KW].unsqueeze(1).broadcast_to([P, HG, KW - j0]),
                               start=True, stop=False, skip_group_check=True)
                            nk = min(KW, (t + 1) * Q)
                            q1 = (u // 4) * T + (t + 1) * Q
                            for ql, kl in ((q_hi, k_hi), (q_lo, k_hi), (q_hi, k_lo)):
                                ins = mm(dst[:, :, KW - nk:KW],
                                         ql[:, q1 // Q - 1, :, :].rearrange("p v q -> p (v q)"),
                                         kl[:, :, q1 - nk:q1], start=False, stop=False, skip_group_check=True)
                        ins.then_inc(s_s, 1)

                    g, k = at(sl, s, FF, 1, NP)
                    if g:
                        bank_a_free(A_SPREAD)
                        if k == 0:
                            pe.wait_ge(s_b, b_before(sl, s, 0))
                        mm(bank_a, pick[:, k, :], cT[:, g.par, :], start=True, stop=True).then_inc(s_a_ps, 1)

                    def bank_b_free(place):
                        if not (sl.fixed and b_before(sl, s, place) == 0):
                            pe.wait_ge(s_b, b_before(sl, s, place))

                    g, b = at(sl, s, OT, 4, GB)
                    if g:
                        bank_b_free(B_POST)
                        pe.wait_ge(s_o, g.n * GB + b + 1)
                        for n in range(4):
                            half, j = divmod(n, 2)
                            ins = nc.tensor.transpose(bank_b[:, P * n:P * n + P], o_f[:, j, P * half:P * half + P], ident)
                        ins.then_inc(s_b_ps, 1)
                    g, b = at(sl, s, ON, 4, GB)
                    if g:
                        bank_b_free(B_POST)
                        for half in range(2):
                            ins = nc.tensor.transpose(bank_b[:, P * half:P * half + P], o_n[:, half, :], ident)
                        ins.then_inc(s_b_ps, 1)
                    g, b = at(sl, s, OW, 4, GB)
                    if g:
                        bank_b_free(B_POST)
                        for half in range(2):
                            r = slice(P * half, P * half + P)
                            ins = exact3(bank_b[:, r], oT_hi[:, r], oT_lo[:, r], *w2(WO))
                        ins.then_inc(s_b_ps, 1)
                    g, _ = at(sl, s, CT)
                    if g:
                        bank_b_free(B_POST)
                        pe.wait_ge(s_cb, g.n + 1)
                        for n in range(NT):
                            ins = nc.tensor.transpose(PS[0:E, BANK_B, P * n:P * n + P], comb[:, n, :], ident)
                        ins.then_inc(s_b_ps, 1)

                    g, v = at(sl, s, PV, 1, NU)
                    if g:
                        b, p = divmod(v, 4)
                        if p == 0:
                            if not (g.fixed and g.n == 0 and b == 0):
                                pe.wait_ge(s_o, g.n * GB + b)
                            mm(PS[:, 2, :], zero_bf[:, 0:P], zero_bf[:, :], start=True, stop=False,
                               skip_group_check=True)
                        pe.wait_ge(s_pt, g.n * NU + 4 * b + min(p + 1, 3) + 1)
                        for kb in (2 * p, 2 * p + 1):
                            nq = min(3, NQ - kb)
                            for a in range(HG):
                                pt = probsT[:, b, a, :, :, :].rearrange("p t c q -> p (t c) q")
                                r0, c0 = 64 * (a % 2), T * (a // 2) + Q * kb
                                ins = mm(PS[r0:r0 + 64, 2, c0:c0 + Q * nq],
                                         v_bd[:, g.par, b * NQ + kb, a, :, :].rearrange("p k f -> p (k f)"),
                                         pt[:, 3 * kb + 2:3 * kb + 2 + 2 * nq - 1:2, :],
                                         start=False, stop=(kb == NQ - 1), skip_group_check=True)
                        if p == 3:
                            ins.then_inc(s_o_ps, 1)

                    g, u = at(sl, s, SC, 1, NU)
                    if g:
                        bank_b_free(B_MAX)
                        pe.wait_ge(s_m, g.n * NU + u + 1)
                        nc.tensor.transpose(PS[0:8, BANK_B, 0:P], neg_max[:, :], ident).then_inc(s_b_ps, 1)

                    g, _ = at(sl, s, SH)
                    if g:
                        gate_up(g, NP, 0)

                    g, half = at(sl, s, RP, 1, 2)
                    if g:
                        values(A_LATE, 2 * half + 1)
                    keys(1)
                    g, b = at(sl, s, XT2, 4, GB)
                    if g:
                        bank_a_free(A_LATE)
                        pe.wait_ge(s_xn2, g.n * NT + 2 * b + 2)
                        for n in range(2):
                            ins = nc.tensor.transpose(bank_a[:, P * n:P * n + P], xn2[:, n, :], ident)
                        ins.then_inc(s_a_ps, 1)
                    g, _ = at(sl, s, YT)
                    if g:
                        bank_a_free(A_LATE)
                        pe.wait_ge(s_y, g.n + 1)
                        for n in range(NT):
                            ins = nc.tensor.transpose(bank_a[:, P * n:P * n + P], y_f[:, P * n:P * n + P], ident)
                        ins.then_inc(s_a_ps, 1)

                    g, k = at(sl, s, DN, 1, NP)
                    if g:
                        if k == 0 and not (g.fixed and g.n == 0):
                            pe.wait_ge(s_y, g.n)
                        pe.wait_ge(s_h, g.n * NP + k + 1)
                        if k == 1:
                            pe.wait_ge(s_fb, g.n * NF + 1)
                            mm(PS[:, 7, :], wd[:, NP, :], hs[:, :], start=False, stop=False)
                        ins = mm(PS[:, 7, :], wd[:, k, :], hh[:, k % 2, :], start=(k == 0), stop=(k == NP - 1))
                        if k == NP - 1:
                            ins.then_inc(s_dn, 1)

            run_slots(pe, slot)


def kernel(**inputs):
    import numpy as np
    import concourse.bacc as _bacc
    from concourse import mybir as _mybir
    from concourse.bass_utils import run_bass_kernel_spmd as _run

    a = {k[3:]: np.asarray(v) for k, v in inputs.items()}
    both = [np.concatenate([a[f"ffn_w_{n}"].transpose(1, 0, 2).reshape(C, E * M), a[f"ffn_sw_{n}"]], axis=1)
            for n in ("gate", "up")]
    lanes = np.arange(P)

    cst = np.zeros((P, CONST_COLS), np.float32)

    def put(name, value):
        cst[:value.shape[0], CONST_AT[name]:CONST_AT[name] + CONSTS[name]] = value.reshape(value.shape[0], -1)

    put("ident", np.eye(P))
    put("headrow", (lanes[:, None] // D) % 4 == np.arange(4))
    put("grouprow", lanes[:, None] // 32 == np.arange(HG))
    put("headcol", lanes[:, None] // 32 == np.arange(32) // D)
    unit = np.repeat(np.eye(32)[:, :8, None], KW, axis=2)
    put("unit", np.concatenate([unit, unit]))
    pick = 0.5 * np.repeat(np.eye(32)[:, :E], M, axis=1)
    put("pick", np.concatenate([pick, pick]))
    i, j = np.arange(Q)[:, None], np.arange(KW)
    seen = (j > i) & (j <= i + W)
    put("band", np.where(np.stack([seen, seen & (j >= W)], axis=1), 0.0, -1e30))
    put("spreadq", (lanes[:, None, None] == np.arange(4)[:, None] * 32 + lanes % 32))
    put("ident4", np.tile(np.eye(Q), 4))
    put("lower", np.tile((np.arange(N_GROUP)[None, :] < np.arange(N_GROUP)[:, None]).reshape(1, -1), (P, 1)))

    arrays = {
        "x": a["attn_x"].reshape(B * T, C),
        "wq": a["attn_Wq"].T, "wk": a["attn_Wk"].T, "wv": a["attn_Wv"].T, "wo": a["attn_Wo"].T,
        "gate_w": a["ffn_gate_kernel"], "gate_b": a["ffn_gate_bias"],
        "w_gu": np.concatenate(both, axis=1),
        "w_down": a["ffn_w_down"].reshape(E * M, C), "sw_down": a["ffn_sw_down"],
        "consts": cst,
    }
    arrays = {k: np.ascontiguousarray(v) for k, v in arrays.items()}
    nc = _bacc.Bacc("TRN2", target_bir_lowering=False, num_devices=1)
    args = [nc.dram_tensor(k, v.shape, _mybir.dt.from_np(v.dtype), kind="ExternalInput").ap() for k, v in arrays.items()]
    out = nc.dram_tensor("out", (B * T, C), _mybir.dt.float32, kind="ExternalOutput").ap()
    preln_block_kernel(nc, *args, out)
    r = _run(nc, [arrays], core_ids=[0])
    return r.results[0]["out"].reshape(B, T, C)
```

```python
from collections import namedtuple
from contextlib import ExitStack

import concourse.bass as bass
from concourse import mybir

F32 = mybir.dt.float32
F32R = mybir.dt.float32r
BF16 = mybir.dt.bfloat16
ALU = mybir.AluOpType
ACT = mybir.ActivationFunctionType
AX_X = mybir.AxisListType.X

P = 128
B, T, C = 32, 256, 128
H, D, W = 16, 8, 64
E, M = 16, 64
TOP_K, N_GROUP, TOPK_GROUP, ROUTE_SCALE = 4, 4, 2, 2.5
EPS = 1e-5
Q_SCALE = float(D) ** -0.5

GB = 2
NG = B // GB
TOK = GB * T
NT = TOK // P
Q = 32
NQ = T // Q
NSB = GB * NQ
HG = H // 4
KW = W + Q
NU = NSB // 2
NP = E // 2
NF = NP + 1
assert NU == NP == 8
STEPS = 8


LN1 = 0
XT = 1
QP, VP, RP = 2, 3, 4
QC = (4, 8)
QC_LOW = (4, 9)
KP = (6, 8)
KC = (7, 10)
SC = 8
TR = 9
PV = 11
OE = 14
OT, ON, OW = 14, 15, 16
LN2 = 17
XT2 = 19
LG = 24
RT = 24
CT = 27
SH = 27
FF = 28
SP_BUFS = 4
DN = 29
YE = 36
YT = 39

RING = (3, 6)
EARLY, POST, WEIGHTS, LATE = range(4)
KEY_PLACE = (EARLY, LATE)
USES = sorted([(stage % STEPS, place, stage) for place, stages in (
    (EARLY, (VP, RP, RP + 1, KP[0], YT, LG)), (LATE, (XT, QP, RP, RP + 1, KP[1], XT2, XT2 + 4)),
    (POST, (OT, OT + 4, ON, ON + 4, OW, OW + 4)), (WEIGHTS, (CT,)))
    for stage in stages])
assert len({use[:2] for use in USES}) == len(USES)
SPLIT = (VP, *KP, XT, QP, XT2, XT2 + 4, ON, ON + 4)

LOOP_FIRST, LOOP_END = 6, NG
LAST_SLOT = NG - 1 + YT // STEPS

Slot = namedtuple("Slot", "n par fixed pair")
Use = namedtuple("Use", "bank before high")
Group = namedtuple("Group", "n par fixed")


def at(slot, s, stage, stride=1, count=1):
    for k in range(count):
        d = stage + k * stride
        if d % STEPS == s:
            off = d // STEPS
            if slot.fixed and not 0 <= slot.n - off < NG:
                return None, 0
            return Group(slot.n - off, (slot.par + off) % 2, slot.fixed), k
    return None, 0


def shared_use(slot, s, place):
    def before(n, s, place):
        return [stage for m in range(n + 1) for a, b, stage in USES
                if 0 <= m - stage // STEPS < NG and (m < n or (a, b) < (s, place))]

    def counts(stages, bank):
        mine = stages[bank::2]
        return len(mine), sum(stage in SPLIT for stage in mine)

    stages = before(slot.n if slot.fixed else LOOP_FIRST + slot.par, s, place)
    bank = len(stages) % 2
    count, high = counts(stages, bank)
    if not slot.fixed:
        first, after = (counts(before(n, 0, 0), bank) for n in (LOOP_FIRST, LOOP_FIRST + 2))
        turns = slot.pair - LOOP_FIRST // 2
        count, high = turns * (after[0] - first[0]) + count, turns * (after[1] - first[1]) + high
    return Use(bank, count, high)


def slot_before(slot):
    if slot.fixed:
        return Slot(slot.n - 1, 1 - slot.par, True, None)
    return Slot(slot.n - 1, 1 - slot.par, False, slot.pair - (slot.par == 0))


def turn(g):
    return (g.n - g.par) * 8 + 16


def spread_turn(g, k):
    return 32 * (g.n * (NP // SP_BUFS) + k // SP_BUFS + 1)


CONSTS = {"ident": P, "headrow": 4, "grouprow": HG, "headcol": 32, "lower": N_GROUP * N_GROUP,
          "band": 2 * KW, "ident4": P, "spreadq": 4 * P}
CONST_AT, CONST_COLS = {}, 0
for _name, _cols in CONSTS.items():
    CONST_AT[_name] = CONST_COLS
    CONST_COLS += _cols
KEPT = CONST_AT["band"]
WQ, WK, WV, WO, GK = 0, C, 2 * C, 3 * C, 4 * C
WG = GK + E
WU = WG + NF * P
W_COLS = WU + NF * P
LOADS, FFN_LOADS = 4, 3
PREPARE = 4
ORDER_PER_SLOT = 5
ROUTING_PARTS = 18
ROUTING_PLACES = 7


def preln_block_kernel(nc, x, w_att, gate_b, w_gu, w_down, sw_down, consts, out):
    with ExitStack() as ctx:
        def sb(name, shape, dt=F32):
            return ctx.enter_context(nc.sbuf_tensor(name, shape, dt))

        def sem(name):
            return ctx.enter_context(nc.semaphore(name))

        cst = sb("cst", [P, KEPT])
        w_hi = sb("w_hi", [P, W_COLS], F32R)
        w_lo = sb("w_lo", [P, W_COLS], F32R)
        wd = sb("wd", [P, NF, C])
        band = sb("band", [P, 2, KW], BF16)
        ident4 = sb("ident4", [P, P], BF16)
        spreadq = sb("spreadq", [P, 4, P], F32R)
        zero_bf = sb("zero_bf", [1, 512], BF16)
        bias_b = sb("bias_b", [P, E])
        holder = sb("holder", [P, 1])
        X = sb("X", [P, 2, NT, C])
        X2 = sb("X2", [P, 2, NT, C])
        st1 = sb("st1", [P, NT, 6])
        mv1 = sb("mv1", [P, NT, 2])
        ve1 = sb("ve1", [P, NT])
        rs1 = sb("rs1", [P, NT])
        st2 = sb("st2", [P, 2, 6])
        mv2 = sb("mv2", [P, 2, 2])
        ve2 = sb("ve2", [P, 2])
        rs2 = sb("rs2", [P, 2])
        half_neg = sb("half_neg", [P, NT])
        eps = sb("eps", [P, NT])
        xT_hi = sb("xT_hi", [P, TOK], F32R)
        xT_lo = sb("xT_lo", [P, TOK], F32R)
        qr_hi = sb("qr_hi", [P, TOK], F32R)
        qr_lo = sb("qr_lo", [P, TOK], F32R)
        q_hi = sb("q_hi", [P, NSB, 4, Q], F32R)
        q_lo = sb("q_lo", [P, NSB, 4, Q], F32R)
        kr_hi = sb("kr_hi", [P, T], F32R)
        kr_lo = sb("kr_lo", [P, T], F32R)
        k_hi = sb("k_hi", [P, HG, TOK], F32R)
        k_lo = sb("k_lo", [P, HG, TOK], F32R)
        v_hi = sb("v_hi", [P, NT, C], F32R)
        v_lo = sb("v_lo", [P, NT, C], F32R)
        v_bd = sb("v_bd", [P, 2, NSB, HG, 2, 32])
        neg_max = sb("neg_max", [P, 2, HG])
        probs = sb("probs", [P, 2, 2, HG, KW])
        probsT = sb("probsT", [P, 2, HG, NQ, 3, Q])
        o_f = sb("o_f", [P, 2, T])
        o_rs = sb("o_rs", [P, 8, 4])
        o_n = sb("o_n", [P, 2, P])
        oT_hi = sb("oT_hi", [P, T], F32R)
        oT_lo = sb("oT_lo", [P, T], F32R)
        H2 = sb("H2", [P, 2, NT, C])
        OUT = sb("OUT", [P, 2, NT, C])
        xn2 = sb("xn2", [P, 2, C])
        x2_hi = sb("x2_hi", [P, 2, TOK], F32R)
        x2_lo = sb("x2_lo", [P, 2, TOK], F32R)
        th_r = sb("th_r", [P, NT * E])
        sc = sb("sc", [P, NT * E])
        pair = sb("pair", [P, NT * N_GROUP, 6])
        gs = sb("gs", [P, NT * N_GROUP])
        g_gt = sb("g_gt", [P, NT, N_GROUP, N_GROUP])
        g_eq = sb("g_eq", [P, NT, N_GROUP, N_GROUP])
        g_rank = sb("g_rank", [P, NT * N_GROUP])
        ms = sb("ms", [P, NT, E])
        m8 = sb("m8", [P, NT, 8])
        e_gt = sb("e_gt", [P, NT, E])
        e_eq = sb("e_eq", [P, NT, E])
        cum = sb("cum", [P, 2, NT, 8 + E])
        ms_w = sb("ms_w", [P, NT, E])
        larger = sb("larger", [P, NT, 3])
        w_pair = sb("w_pair", [P, NT, 2])
        w_sum = sb("w_sum", [P, NT])
        comb = sb("comb", [P, NT, E])
        cT = sb("cT", [E, TOK])
        th = sb("th", [P, TOK])
        fa = sb("fa", [P, TOK])
        gate = sb("gate", [P, 2, TOK])
        tu = sb("tu", [P, 2, TOK])
        spread = sb("spread", [P, SP_BUFS, TOK])
        hh = sb("hh", [P, 2, TOK])
        hs = sb("hs", [P, TOK])
        gate2 = sb("gate2", [P, TOK])
        y_f = sb("y_f", [P, TOK])
        spare = probsT[:, :, :, :, :, :].rearrange("p b g t c q -> p (b g t c q)")
        stage = spare[:, 0:W_COLS]
        cst_stage = spare[:, W_COLS:W_COLS + CONST_COLS - KEPT]

        weights_t = nc.dram_tensor("weights_by_expert", (2, E, TOK), F32, kind="Internal").ap()

        PS = ctx.enter_context(nc.psum_tensor("PS", [P, 8, 512], F32))

        def const(name, rows=P):
            at_ = CONST_AT[name]
            if at_ >= KEPT:
                return cst_stage[0:rows, at_ - KEPT:at_ - KEPT + CONSTS[name]]
            return cst[0:rows, at_:at_ + CONSTS[name]]

        ident = const("ident")
        headrow = const("headrow")
        grouprow = const("grouprow")
        headcol = const("headcol")
        lower = const("lower").rearrange("p (i j) -> p i j", i=N_GROUP)

        def tiles(ap):
            return ap.rearrange("p (n c) -> p n c", c=C)

        def blocks(ap):
            return ap.rearrange("p (a q) -> p a q", q=Q)

        s_w = sem("first_weights_loaded")
        s_wf = sem("ffn_weights_loaded")
        s_cst = sem("constants_ready")
        s_ones = sem("ones_beside_values")
        s_x = [sem("x_even_loaded"), sem("x_odd_loaded")]
        s_x2 = [sem("x_again_even_loaded"), sem("x_again_odd_loaded")]
        s_cp = [sem("h2_even_copied"), sem("h2_odd_copied")]
        s_st = [sem("even_stored"), sem("odd_stored")]
        s_mv1 = sem("mean_var1_ready")
        s_mv2 = sem("mean_var2_ready")
        s_rs1 = sem("rstd1_ready")
        s_rs2 = sem("rstd2_ready")
        s_pool = sem("pool_order")
        s_dve = sem("dve_order")
        s_xn1 = sem("xn1_ready")
        s_xn2 = sem("xn2_ready")
        s_filled = [sem("shared0_filled"), sem("shared1_filled")]
        s_high = [sem("shared0_high_out"), sem("shared1_high_out")]
        s_taken = [sem("shared0_taken"), sem("shared1_taken")]
        s_q_hi = sem("q_high_copies_ready")
        s_q_lo = sem("q_low_copies_ready")
        s_k_hi = sem("k_high_copies_ready")
        s_k_lo = sem("k_low_copies_ready")
        s_xc = sem("centred1_ready")
        s_xc2 = sem("centred2_ready")
        s_s = sem("scores_ready")
        s_m = sem("neg_max_ready")
        s_p = sem("probs_ready")
        s_pt = sem("probsT_ready")
        s_o_ps = sem("o_in_psum")
        s_o = sem("o_ready")
        s_rt = sem("routing_parts_done")
        s_cb = sem("combine_ready")
        s_g = sem("gate_in_psum")
        s_u = sem("up_in_psum")
        s_th = sem("tanh_ready")
        s_spread = [sem(f"spread{n}_loaded") for n in range(SP_BUFS)]
        s_wt = sem("weights_by_expert_in_dram")
        s_gate = sem("gate_copied")
        s_fa = sem("shared_silu2_ready")
        s_tu = sem("up_taken")
        s_g2 = sem("weight_times_gate_ready")
        s_h = sem("hidden_ready")
        s_dn = sem("ffn_in_psum")
        s_y = sem("ffn_ready")

        def taken(eng, slot, s, place):
            use = shared_use(slot, s, place)
            eng.wait_ge(s_taken[use.bank], use.before + 1)

        def filled(eng, slot, s, place):
            use = shared_use(slot, s, place)
            eng.wait_ge(s_filled[use.bank], use.before + 1)
            return use.bank, PS[:, RING[use.bank], :]

        x_t = x.rearrange("(g n p) c -> g p n c", n=NT, p=P)
        out_t = out.rearrange("(g n p) c -> g p n c", n=NT, p=P)

        def run_slots(eng, body):
            for n in range(LOOP_FIRST):
                body(Slot(n, n % 2, True, None))
            with eng.Fori(LOOP_FIRST // 2, LOOP_END // 2) as pair_of_slots:
                body(Slot(pair_of_slots * 2, 0, False, pair_of_slots))
                body(Slot(pair_of_slots * 2 + 1, 1, False, pair_of_slots))
            for n in range(LOOP_END, LAST_SLOT + 1):
                body(Slot(n, n % 2, True, None))

        block = ctx.enter_context(nc.Block())

        @block.sync
        def _(sp):
            sp.dma_start(X[:, 0, :, :], x_t[0]).then_inc(s_x[0], 16)
            sp.dma_start(cst[:, :], consts[:, 0:KEPT]).then_inc(s_w, 16)
            sp.dma_start(stage[:, 0:WG], w_att).then_inc(s_w, 16)
            sp.dma_start(cst_stage, consts[:, KEPT:CONST_COLS]).then_inc(s_w, 16)
            sp.dma_start(bias_b[:, :], gate_b.partition_broadcast(P)).then_inc(s_w, 16)
            sp.dma_start(stage[:, WG:W_COLS], w_gu).then_inc(s_wf, 16)
            sp.dma_start(wd[:, 0:NP, :], w_down.rearrange("(j p) c -> p j c", p=P)).then_inc(s_wf, 16)
            sp.dma_start(wd[:, NP, :], sw_down).then_inc(s_wf, 16)

            def load_x(sl, g):
                if not (g.fixed and g.n < 2):
                    taken(sp, slot_before(sl), XT % STEPS, LATE)
                sp.dma_start(X[:, g.par, :, :], x_t[g.n]).then_inc(s_x[g.par], 16)

            def spread_out(g, k):
                for e in range(2):
                    sp.dma_start(spread[M * e:M * e + M, k % SP_BUFS, :],
                                 weights_t[g.par, 2 * k + e].partition_broadcast(M)
                                 ).then_inc(s_spread[k % SP_BUFS], 16)

            def slot(sl):
                if not (sl.fixed and not 0 < sl.n < NG):
                    load_x(sl, Group(sl.n, sl.par, sl.fixed))
                for s in range(STEPS):
                    g, _ = at(sl, s, 25)
                    if g:
                        taken(sp, slot_before(sl), (OW + 4) % STEPS, POST)
                        if not (g.fixed and g.n < 2):
                            sp.wait_ge(s_st[g.par], turn(g) - 16)
                        sp.dma_start(OUT[:, g.par, :, :], H2[:, g.par, :, :]).then_inc(s_cp[g.par], 16)
                    g, _ = at(sl, s, 12)
                    if g:
                        if not (g.fixed and g.n < 2):
                            taken(sp, slot_before(sl), (OW + 4) % STEPS, POST)
                        sp.dma_start(X2[:, g.par, :, :], x_t[g.n]).then_inc(s_x2[g.par], 16)
                    g, _ = at(sl, s, CT)
                    if g:
                        taken(sp, sl, CT % STEPS, WEIGHTS)
                        sp.dma_start(weights_t[g.par], cT[:, :]).then_inc(s_wt, 16)
                        if not (g.fixed and g.n == 0):
                            sp.wait_ge(s_h, g.n * NP)
                        sp.wait_ge(s_wt, 16 * g.n + 16)
                        for k in range(SP_BUFS):
                            spread_out(g, k)
                    g, n = at(sl, s, FF + 1, 1, NP - SP_BUFS)
                    if g:
                        sp.wait_ge(s_h, g.n * NP + n + 1)
                        spread_out(g, n + SP_BUFS)
                    g, _ = at(sl, s, YT)
                    if g:
                        taken(sp, sl, YT % STEPS, EARLY)
                        sp.dma_start(out_t[g.n], OUT[:, g.par, :, :]).then_inc(s_st[g.par], 16)

            run_slots(sp, slot)
            for par in range(2):
                sp.wait_ge(s_st[par], 16 * NG // 2)

        @block.gpsimd
        def _(pool):
            tt = nc.gpsimd.tensor_tensor
            nc.gpsimd.memset(half_neg[:, :], -0.5).then_inc(s_pool, 1)
            nc.gpsimd.memset(eps[:, :], EPS).then_inc(s_pool, 1)
            pool.wait_ge(s_pool, 2)

            def slot(sl):
                for s in range(STEPS):
                    if sl.fixed and sl.n == 0 and s == 1:
                        pool.wait_ge(s_w, 16 * LOADS)
                    g, _ = at(sl, s, LN1)
                    if g:
                        pool.wait_ge(s_mv1, g.n + 1)
                        wide = [P, NT, C]
                        tt(ve1[:, :], mv1[:, :, 1], eps[:, :], ALU.add).then_inc(s_rs1, 1)
                        tt(X[:, g.par, :, :], X[:, g.par, :, :], mv1[:, :, 0:1].broadcast_to(wide),
                           ALU.subtract).then_inc(s_xc, 1)
                        pool.wait_ge(s_rs1, 2 * g.n + 1)
                        tt(rs1[:, :], ve1[:, :], half_neg[:, :], ALU.pow).then_inc(s_rs1, 1)
                        pool.wait_ge(s_xc, g.n + 1)
                        pool.wait_ge(s_rs1, 2 * g.n + 2)
                        tt(X[:, g.par, :, :], X[:, g.par, :, :], rs1[:, :].unsqueeze(2).broadcast_to(wide),
                           ALU.mult).then_inc(s_xn1, 1)
                    for b in range(GB):
                        g, pair_ = at(sl, s, QC_LOW[b], 1, 2)
                        if not g:
                            continue
                        if pair_ == 0:
                            if b == 0:
                                taken(pool, sl, QP % STEPS, LATE)
                            if not (g.fixed and g.n == 0):
                                pool.wait_ge(s_s, 2 * ((g.n - 1) * NU + 4 * b + 4))
                        for a in (2 * pair_, 2 * pair_ + 1):
                            tt(q_lo[:, NQ * b:NQ * b + NQ, a, :], blocks(qr_lo[:, T * b:T * b + T].bitcast(F32)),
                               headrow[:, a:a + 1].unsqueeze(2).broadcast_to([P, NQ, Q]), ALU.mult).then_inc(s_q_lo, 1)
                    for b in range(GB):
                        g, _ = at(sl, s, KC[b])
                        if g:
                            taken(pool, sl, KP[b] % STEPS, KEY_PLACE[b])
                            if not (g.fixed and g.n == 0):
                                pool.wait_ge(s_s, 2 * ((g.n - 1) * NU + 4 * b + 4))
                            for a in range(HG):
                                tt(k_lo[:, a, T * b:T * b + T], kr_lo[:, :].bitcast(F32),
                                   grouprow[:, a:a + 1].broadcast_to([P, T]), ALU.mult).then_inc(s_k_lo, 1)
                    g, k = at(sl, s, FF, 1, NP)
                    if g:
                        if not (g.fixed and g.n == 0 and k == 0):
                            pool.wait_ge(s_h, g.n * NP + k)
                        pool.wait_ge(s_gate, g.n * NP + k + 1)
                        pool.wait_ge(s_spread[k % SP_BUFS], spread_turn(g, k))
                        tt(gate2[:, :], gate[:, k % 2, :], spread[:, k % SP_BUFS, :], ALU.mult).then_inc(s_g2, 1)
                        pool.wait_ge(s_g2, g.n * NP + k + 1)
                        pool.wait_ge(s_tu, g.n * NF + k + 2)
                        tt(hh[:, k % 2, :], gate2[:, :], tu[:, k % 2, :], ALU.mult).then_inc(s_h, 1)
                    g, b = at(sl, s, LN2, 4, GB)
                    if g:
                        turns = g.n * GB + b
                        pool.wait_ge(s_mv2, turns + 1)
                        wide = [P, 2, C]
                        tt(ve2[:, :], mv2[:, :, 1], eps[:, 0:2], ALU.add).then_inc(s_rs2, 1)
                        if b == 1:
                            taken(pool, sl, XT2 % STEPS, LATE)
                        elif not (g.fixed and g.n == 0):
                            taken(pool, slot_before(sl), (XT2 + 4) % STEPS, LATE)
                        tt(xn2[:, :, :], H2[:, g.par, 2 * b:2 * b + 2, :], mv2[:, :, 0:1].broadcast_to(wide),
                           ALU.subtract).then_inc(s_xc2, 1)
                        pool.wait_ge(s_rs2, 2 * turns + 1)
                        tt(rs2[:, :], ve2[:, :], half_neg[:, 0:2], ALU.pow).then_inc(s_rs2, 1)
                        pool.wait_ge(s_xc2, turns + 1)
                        pool.wait_ge(s_rs2, 2 * turns + 2)
                        tt(xn2[:, :, :], xn2[:, :, :], rs2[:, :].unsqueeze(2).broadcast_to(wide),
                           ALU.mult).then_inc(s_xn2, 1)

            run_slots(pool, slot)

        @block.scalar
        def _(act):
            def copy(dst, src, **kw):
                return nc.scalar.activation(dst, src, ACT.Copy, **kw)

            act.wait_ge(s_w, 16 * LOADS)
            copy(w_hi[:, 0:WG], stage[:, 0:WG]).then_inc(s_cst, 1)

            def slot(sl):
                for s in range(STEPS):
                    if sl.fixed and sl.n == 0 and s in (5, 6):
                        nc.scalar.activation(v_bd[:, s - 5, :, :, 1, :].rearrange("p n g f -> p (n g) f"),
                                             headcol.unsqueeze(1).broadcast_to([P, NSB * HG, 32]),
                                             ACT.Copy).then_inc(s_ones, 1)
                    if sl.fixed and sl.n == 0 and s == PREPARE:
                        act.wait_ge(s_wf, 16 * FFN_LOADS)
                        act.wait_ge(s_cst, 2)
                        copy(w_hi[:, WG:W_COLS], stage[:, WG:W_COLS]).then_inc(s_cst, 1)
                    g, b = at(sl, s, OE, 4, GB)
                    if g:
                        act.wait_ge(s_o_ps, g.n * GB + b + 1)
                        copy(o_f[:, :, :], PS[:, 2, :].rearrange("p (j q) -> p j q", j=2)).then_inc(s_o, 1)

                    g, _ = at(sl, s, VP)
                    if g:
                        side, bank = filled(act, sl, s, EARLY)
                        copy(v_hi[:, :, :], tiles(bank)).then_inc(s_high[side], 1)
                    def keys(b):
                        g, _ = at(sl, s, KP[b])
                        if g:
                            side, bank = filled(act, sl, s, KEY_PLACE[b])
                            if not (g.fixed and g.n == 0 and b == 0):
                                act.wait_ge(s_k_hi, g.n * GB + b)
                            copy(kr_hi[:, :], bank[:, 0:T]).then_inc(s_high[side], 1)

                    keys(0)
                    g, _ = at(sl, s, LG)
                    if g:
                        side, bank = filled(act, sl, s, EARLY)
                        nc.scalar.activation(th_r[:, :], bank[:, 0:NT * E], ACT.Tanh,
                                             scale=0.5).then_inc(s_taken[side], 1)
                    g, k = at(sl, s, FF, 1, NP)
                    if g:
                        act.wait_ge(s_g, g.n * NF + k + 2)
                        nc.scalar.activation(th[:, :], PS[:, 4, :], ACT.Tanh, scale=0.5).then_inc(s_th, 1)
                        copy(gate[:, k % 2, :], PS[:, 4, :]).then_inc(s_gate, 1)

                    g, b = at(sl, s, ON, 4, GB)
                    if g:
                        side, bank = filled(act, sl, s, POST)
                        copy(oT_hi[:, :], bank[:, 0:T]).then_inc(s_high[side], 1)
                    g, _ = at(sl, s, CT)
                    if g:
                        side, bank = filled(act, sl, s, WEIGHTS)
                        if not (g.fixed and g.n == 0):
                            act.wait_ge(s_wt, 16 * g.n)
                        copy(cT[:, :], bank[0:E, :], scale=0.5).then_inc(s_taken[side], 1)
                    g, _ = at(sl, s, SH)
                    if g:
                        act.wait_ge(s_g, g.n * NF + 1)
                        if not (g.fixed and g.n == 0):
                            act.wait_ge(s_fa, g.n)
                        nc.scalar.activation(th[:, :], PS[:, 4, :], ACT.Tanh, scale=0.5).then_inc(s_th, 1)
                    keys(1)
                    g, _ = at(sl, s, QP)
                    if g:
                        if not (g.fixed and g.n == 0):
                            act.wait_ge(s_q_hi, g.n * GB)
                        side, bank = filled(act, sl, s, LATE)
                        copy(qr_hi[:, :], bank, scale=Q_SCALE).then_inc(s_high[side], 1)
                    g, _ = at(sl, s, XT)
                    if g:
                        side, bank = filled(act, sl, s, LATE)
                        copy(xT_hi[:, :], bank).then_inc(s_high[side], 1)
                    g, b = at(sl, s, XT2, 4, GB)
                    if g:
                        side, bank = filled(act, sl, s, LATE)
                        copy(x2_hi[:, g.par, T * b:T * b + T], bank[:, 0:T]).then_inc(s_high[side], 1)
                    g, u = at(sl, s, SC, 1, NU)
                    if g:
                        j0 = Q if u % 4 == 0 else 0
                        if u >= 2 or not (g.fixed and g.n == 0):
                            act.wait_ge(s_pt, g.n * NU + u - 1)
                        for tt in range(2):
                            act.wait_ge(s_m, 2 * (g.n * NU + u) + tt + 1)
                            for a in range(HG):
                                ins = nc.scalar.activation(
                                    probs[:, u % 2, tt, a, j0:KW], PS[:, tt, a * KW + j0:a * KW + KW], ACT.Exp,
                                    bias=neg_max[:, tt, a:a + 1])
                            ins.then_inc(s_p, 1)
                    for b in range(GB):
                        g, pair_ = at(sl, s, QC[b], 1, 2)
                        if not g:
                            continue
                        if pair_ == 0:
                            if b == 0:
                                taken(act, sl, QP % STEPS, LATE)
                            if not (g.fixed and g.n == 0):
                                act.wait_ge(s_s, 2 * ((g.n - 1) * NU + 4 * b + 4))
                        for a in (2 * pair_, 2 * pair_ + 1):
                            ins = copy(q_hi[:, NQ * b:NQ * b + NQ, a, :],
                                       blocks(qr_hi[:, T * b:T * b + T].bitcast(F32)), scale=headrow[:, a:a + 1])
                        if pair_ == 1:
                            ins.then_inc(s_q_hi, 1)
                    for b in range(GB):
                        g, _ = at(sl, s, KC[b])
                        if g:
                            taken(act, sl, KP[b] % STEPS, KEY_PLACE[b])
                            if not (g.fixed and g.n == 0):
                                act.wait_ge(s_s, 2 * ((g.n - 1) * NU + 4 * b + 4))
                            for a in range(HG):
                                ins = copy(k_hi[:, a, T * b:T * b + T], kr_hi[:, :].bitcast(F32),
                                           scale=grouprow[:, a:a + 1])
                            ins.then_inc(s_k_hi, 1)
                    g, _ = at(sl, s, YE)
                    if g:
                        act.wait_ge(s_dn, g.n + 1)
                        copy(y_f[:, :], PS[:, 7, :]).then_inc(s_y, 1)

            run_slots(act, slot)

        @block.vector
        def _(dve):
            v_ = nc.vector
            v_.memset(zero_bf[:, :], 0.0)
            v_.memset(cum[:, :, :, :], 0.0)
            order = {"before": 0, "done": 0}

            def link(sl, ins):
                order["done"] += 1
                ins.then_inc(s_dve, 1)
                loop = 0 if sl.fixed else (sl.n - LOOP_FIRST) * ORDER_PER_SLOT
                dve.wait_ge(s_dve, order["before"] + loop + order["done"])

            def split_low(dst, src, high):
                return v_.tensor_tensor(dst, src, high.bitcast(F32), ALU.subtract)

            def high_out(sl, s, place):
                use = shared_use(sl, s, place)
                dve.wait_ge(s_high[use.bank], use.high + 1)
                return use.bank, PS[:, RING[use.bank], :]

            def stats(sl, src, n, st, mv):
                for a in range(n):
                    ins = v_.bn_stats(st[:, a, :], src[:, a, :])
                link(sl, ins)
                v_.memset(holder[:, :], 0.0)
                for a in range(n):
                    ins = v_.bn_aggr(mv[:, a, :], st[:, a, :])
                return ins

            def routing(sl, s, place):
                g, _ = at(sl, s, RT, 1, 3)
                if not g:
                    return
                part = (s - RT % STEPS) * ROUTING_PLACES + place - 2
                if not 0 <= part <= ROUTING_PARTS:
                    return
                if part == 0:
                    taken(dve, sl, s, EARLY)
                else:
                    dve.wait_ge(s_rt, g.n * ROUTING_PARTS + part)
                full, square = [P, NT, E], [P, NT, N_GROUP, N_GROUP]
                sc3 = sc[:, :].rearrange("p (n e) -> p n e", n=NT)
                s4 = sc[:, :].rearrange("p (n e) -> p n e", e=4)
                gs3 = gs[:, :].rearrange("p (n g) -> p n g", n=NT)
                fourth = m8[:, :, TOP_K - 1:TOP_K]
                tt, count = v_.tensor_tensor, cum[:, :, :, 8:8 + E]
                if part == 0:
                    ins = v_.tensor_scalar(sc[:, :], th_r[:, :], 0.5, 0.5, ALU.mult, ALU.add)
                elif part == 1:
                    ins = tt(sc3, sc3, bias_b[:, :].unsqueeze(1).broadcast_to(full), ALU.add)
                elif part == 2:
                    tt(pair[:, :, 0:3], s4[:, :, 0:3], s4[:, :, 1:4], ALU.add)
                    tt(pair[:, :, 3:5], s4[:, :, 0:2], s4[:, :, 2:4], ALU.add)
                    ins = tt(pair[:, :, 5:6], s4[:, :, 0:1], s4[:, :, 3:4], ALU.add)
                elif part == 3:
                    ins = v_.tensor_reduce(gs[:, :], pair[:, :, :], AX_X, ALU.max)
                elif part == 4:
                    g_j, g_i = gs3.unsqueeze(2).broadcast_to(square), gs3.unsqueeze(3).broadcast_to(square)
                    tt(g_gt[:, :, :, :], g_j, g_i, ALU.is_gt)
                    ins = tt(g_eq[:, :, :, :], g_j, g_i, ALU.is_equal)
                elif part == 5:
                    ins = tt(g_eq[:, :, :, :], g_eq[:, :, :, :], lower.unsqueeze(1).broadcast_to(square), ALU.mult)
                elif part == 6:
                    ins = tt(g_gt[:, :, :, :], g_gt[:, :, :, :], g_eq[:, :, :, :], ALU.add)
                elif part == 7:
                    ins = v_.tensor_reduce(g_rank[:, :], g_gt[:, :, :, :].rearrange("p n i j -> p (n i) j"),
                                           AX_X, ALU.add)
                elif part == 8:
                    ins = v_.scalar_tensor_tensor(
                        ms[:, :, :].rearrange("p n (g e) -> p (n g) e", g=N_GROUP),
                        g_rank[:, :].unsqueeze(2).broadcast_to([P, NT * N_GROUP, 4]), float(TOPK_GROUP), s4,
                        ALU.is_lt, ALU.mult)
                elif part == 9:
                    v_.memset(holder[:, :], 0.0)
                    for n in range(NT):
                        ins = v_.max(m8[:, n, :], ms[:, n, :])
                elif part == 10:
                    tt(e_gt[:, :, :], ms[:, :, :], fourth.broadcast_to(full), ALU.is_gt)
                    tt(e_eq[:, :, :], ms[:, :, :], fourth.broadcast_to(full), ALU.is_equal)
                    tt(larger[:, :, :], m8[:, :, 0:3], fourth.broadcast_to([P, NT, 3]), ALU.is_gt)
                    tt(w_pair[:, :, :], m8[:, :, 0:2], m8[:, :, 2:4], ALU.add)
                    ins = tt(count[:, 0], ms[:, :, :], fourth.broadcast_to(full), ALU.is_equal)
                elif part == 11:
                    tt(larger[:, :, 0:1], larger[:, :, 0:1], larger[:, :, 1:2], ALU.add)
                    tt(w_sum[:, :].unsqueeze(2), w_pair[:, :, 0:1], w_pair[:, :, 1:2], ALU.add)
                    ins = tt(count[:, 1], count[:, 0], cum[:, 0, :, 7:7 + E], ALU.add)
                elif part == 12:
                    tt(larger[:, :, 0:1], larger[:, :, 0:1], larger[:, :, 2:3], ALU.add)
                    v_.tensor_scalar(w_sum[:, :], w_sum[:, :], 1e-20, None, ALU.add)
                    ins = tt(count[:, 0], count[:, 1], cum[:, 1, :, 6:6 + E], ALU.add)
                elif part == 13:
                    v_.reciprocal(w_sum[:, :], w_sum[:, :])
                    ins = tt(count[:, 1], count[:, 0], cum[:, 0, :, 4:4 + E], ALU.add)
                elif part == 14:
                    v_.scalar_tensor_tensor(ms_w[:, :, :], ms[:, :, :], ROUTE_SCALE,
                                            w_sum[:, :].unsqueeze(2).broadcast_to(full), ALU.mult, ALU.mult)
                    ins = tt(count[:, 0], count[:, 1], cum[:, 1, :, 0:E], ALU.add)
                elif part == 15:
                    ins = tt(count[:, 1], count[:, 0], larger[:, :, 0:1].broadcast_to(full), ALU.add)
                elif part == 16:
                    ins = v_.scalar_tensor_tensor(e_eq[:, :, :], count[:, 1], float(TOP_K), e_eq[:, :, :],
                                                  ALU.is_le, ALU.mult)
                elif part == 17:
                    ins = tt(e_gt[:, :, :], e_gt[:, :, :], e_eq[:, :, :], ALU.add)
                else:
                    tt(comb[:, :, :], e_gt[:, :, :], ms_w[:, :, :], ALU.mult).then_inc(s_cb, 1)
                    return
                ins.then_inc(s_rt, 1)

            def slot(sl):
                order["done"] = 0 if sl.fixed or sl.par == 0 else order["done"]
                if not sl.fixed and sl.par == 1:
                    order["done"] = 0
                for s in range(STEPS):
                    if sl.fixed and sl.n == 0 and s == 1:
                        dve.wait_ge(s_w, 16 * LOADS)
                        v_.tensor_copy(spreadq[:, :, :], const("spreadq").rearrange("p (a k) -> p a k", a=4))
                        v_.tensor_copy(band[:, :, :], const("band").rearrange("p (a k) -> p a k", a=2))
                        v_.tensor_copy(ident4[:, :], const("ident4"))
                        dve.wait_ge(s_cst, 1)
                        v_.tensor_tensor(w_lo[:, 0:WG], stage[:, 0:WG], w_hi[:, 0:WG].bitcast(F32),
                                         ALU.subtract).then_inc(s_cst, 1)
                    if sl.fixed and sl.n == 0 and s == PREPARE:
                        dve.wait_ge(s_cst, 3)
                        v_.tensor_tensor(w_lo[:, WG:W_COLS], stage[:, WG:W_COLS], w_hi[:, WG:W_COLS].bitcast(F32),
                                         ALU.subtract).then_inc(s_cst, 1)
                        dve.wait_ge(s_cst, 4)
                    g, u = at(sl, s, TR, 1, NU)
                    if g:
                        b, t0 = u // 4, 2 * (u % 4)
                        dve.wait_ge(s_p, 2 * (g.n * NU + u + 1))
                        c0 = 1 if u % 4 == 0 else 0
                        for tt in range(2):
                            ins = v_.transpose(
                                probsT[:, b, :, t0 + tt, c0:3, :].rearrange("p g c q -> p g (c q)"),
                                probs[:, u % 2, tt, :, c0 * Q:KW])
                        ins.then_inc(s_pt, 1)

                    routing(sl, s, 0)
                    g, _ = at(sl, s, VP)
                    if g:
                        side, bank = high_out(sl, s, EARLY)
                        split_low(v_lo[:, :, :], tiles(bank), v_hi[:, :, :]).then_inc(s_taken[side], 1)
                    def keys(b):
                        g, _ = at(sl, s, KP[b])
                        if g:
                            side, bank = high_out(sl, s, KEY_PLACE[b])
                            if not (g.fixed and g.n == 0 and b == 0):
                                dve.wait_ge(s_k_lo, HG * (g.n * GB + b))
                            split_low(kr_lo[:, :], bank[:, 0:T], kr_hi[:, :]).then_inc(s_taken[side], 1)

                    g, _ = at(sl, s, YT)
                    if g:
                        side, bank = filled(dve, sl, s, EARLY)
                        dve.wait_ge(s_cp[g.par], turn(g))
                        v_.tensor_tensor(OUT[:, g.par, :, :], tiles(bank), OUT[:, g.par, :, :],
                                         ALU.add).then_inc(s_taken[side], 1)
                    keys(0)

                    def values(place, a):
                        side, bank = filled(dve, sl, s, place)
                        v_.tensor_tensor(v_bd[:, g.par, a:a + 13:4, :, 0, :],
                                         bank.rearrange("p (n g f) -> p n g f", g=HG, f=32),
                                         headcol.unsqueeze(1).unsqueeze(1).broadcast_to([P, NT, HG, 32]),
                                         ALU.mult).then_inc(s_taken[side], 1)

                    g, half = at(sl, s, RP, 1, 2)
                    if g:
                        values(EARLY, 2 * half)

                    g, _ = at(sl, s, LN1)
                    if g:
                        dve.wait_ge(s_x[g.par], turn(g))
                        stats(sl, X[:, g.par, :, :], NT, st1, mv1).then_inc(s_mv1, 1)
                    routing(sl, s, 1)
                    g, k = at(sl, s, FF, 1, NP)
                    if g:
                        dve.wait_ge(s_th, g.n * NF + k + 2)
                        dve.wait_ge(s_u, g.n * NF + k + 2)
                        v_.scalar_tensor_tensor(tu[:, k % 2, :], th[:, :], 1.0, PS[:, 5, :], ALU.add,
                                                ALU.mult).then_inc(s_tu, 1)
                    routing(sl, s, 2)
                    routing(sl, s, 3)
                    g, u = at(sl, s, SC, 1, NU)
                    for tt in range(2):
                        if g:
                            j0 = Q if u % 4 == 0 else 0
                            if not (g.fixed and g.n == 0 and u == 0):
                                dve.wait_ge(s_p, 2 * (g.n * NU + u) + tt - 1)
                            dve.wait_ge(s_s, 2 * (g.n * NU + u) + tt + 1)
                            src = PS[:, tt, 0:HG * KW].rearrange("p (g k) -> p g k", g=HG)
                            v_.tensor_reduce(neg_max[:, tt, :], src[:, :, j0:KW],
                                             AX_X, ALU.max, negate=True).then_inc(s_m, 1)
                        routing(sl, s, 4 + tt)
                    g, b = at(sl, s, LN2, 4, GB)
                    if g:
                        taken(dve, sl, (OW + 4 * b) % STEPS, POST)
                        stats(sl, H2[:, g.par, 2 * b:2 * b + 2, :], 2, st2, mv2).then_inc(s_mv2, 1)

                    g, b = at(sl, s, OT, 4, GB)
                    if g:
                        side, bank = filled(dve, sl, s, POST)
                        o_t = bank.rearrange("p (a k v d) -> p a k v d", k=2, v=4, d=D)
                        link(sl, v_.reciprocal(o_rs[:, :, :], o_t[:, :, 1, :, 0]))
                        v_.tensor_tensor(o_n[:, :, :].rearrange("p n (a v d) -> p (n a) v d", v=4, d=D),
                                         o_t[:, :, 0, :, :],
                                         o_rs[:, :, :].unsqueeze(3).broadcast_to([P, 8, 4, D]),
                                         ALU.mult).then_inc(s_taken[side], 1)
                    g, b = at(sl, s, ON, 4, GB)
                    if g:
                        side, bank = high_out(sl, s, POST)
                        split_low(oT_lo[:, :], bank[:, 0:T], oT_hi[:, :]).then_inc(s_taken[side], 1)
                    g, b = at(sl, s, OW, 4, GB)
                    if g:
                        side, bank = filled(dve, sl, s, POST)
                        dve.wait_ge(s_x2[g.par], turn(g))
                        if b == 0 and not (g.fixed and g.n < 2):
                            dve.wait_ge(s_cp[g.par], turn(g) - 16)
                        v_.tensor_tensor(H2[:, g.par, 2 * b:2 * b + 2, :], tiles(bank[:, 0:T]),
                                         X2[:, g.par, 2 * b:2 * b + 2, :], ALU.add).then_inc(s_taken[side], 1)
                    g, _ = at(sl, s, SH)
                    if g:
                        f = g.n * NF + 1
                        dve.wait_ge(s_th, f)
                        v_.scalar_tensor_tensor(fa[:, :], th[:, :], 1.0, PS[:, 4, :], ALU.add,
                                                ALU.mult).then_inc(s_fa, 1)
                        dve.wait_ge(s_fa, g.n + 1)
                        dve.wait_ge(s_u, f)
                        v_.scalar_tensor_tensor(hs[:, :], fa[:, :], 0.5, PS[:, 5, :], ALU.mult,
                                                ALU.mult).then_inc(s_tu, 1)
                    routing(sl, s, 6)
                    g, half = at(sl, s, RP, 1, 2)
                    if g:
                        values(LATE, 2 * half + 1)
                    keys(1)
                    g, _ = at(sl, s, QP)
                    if g:
                        if not (g.fixed and g.n == 0):
                            dve.wait_ge(s_q_lo, g.n * 8)
                        side, bank = high_out(sl, s, LATE)
                        v_.scalar_tensor_tensor(qr_lo[:, :], bank, Q_SCALE, qr_hi[:, :].bitcast(F32),
                                                ALU.mult, ALU.subtract).then_inc(s_taken[side], 1)
                    g, _ = at(sl, s, XT)
                    if g:
                        side, bank = high_out(sl, s, LATE)
                        split_low(xT_lo[:, :], bank, xT_hi[:, :]).then_inc(s_taken[side], 1)
                    g, b = at(sl, s, XT2, 4, GB)
                    if g:
                        side, bank = high_out(sl, s, LATE)
                        cols = slice(T * b, T * b + T)
                        split_low(x2_lo[:, g.par, cols], bank[:, 0:T], x2_hi[:, g.par, cols]).then_inc(s_taken[side], 1)
                if sl.fixed:
                    order["before"] += order["done"]
                else:
                    assert order["done"] == ORDER_PER_SLOT, order["done"]
                    if sl.par == 1:
                        order["before"] += (LOOP_END - LOOP_FIRST) * ORDER_PER_SLOT

            run_slots(dve, slot)

        @block.tensor
        def _(pe):
            mm = nc.tensor.matmul

            def exact3(dst, l_hi, l_lo, r_hi, r_lo):
                mm(dst, l_hi, r_hi, start=True, stop=False)
                mm(dst, l_lo, r_hi, start=False, stop=False)
                return mm(dst, l_hi, r_lo, start=False, stop=True)

            def w2(n, cols=C):
                return w_hi[:, n:n + cols], w_lo[:, n:n + cols]

            pe.wait_ge(s_w, 16 * LOADS)

            def gate_up(g, j, f):
                if not (g.fixed and g.n == 0 and f == 0):
                    pe.wait_ge(s_tu, g.n * NF + f)
                x2 = x2_hi[:, g.par, :], x2_lo[:, g.par, :]
                if g.fixed and g.n == 0 and f == 0:
                    pe.wait_ge(s_cst, 4)
                    pe.wait_ge(s_wf, 16 * FFN_LOADS)
                if not (g.fixed and g.n * NP + f <= 1):
                    pe.wait_ge(s_gate, g.n * NP + max(f - 1, 0))
                exact3(PS[:, 4, :], *w2(WG + P * j), *x2).then_inc(s_g, 1)
                exact3(PS[:, 5, :], *w2(WU + P * j), *x2).then_inc(s_u, 1)

            def slot(sl):
                for s in range(STEPS):
                    if sl.fixed and sl.n == 0 and s == 2:
                        pe.wait_ge(s_cst, 2)
                    g, v = at(sl, s, PV, 1, NU)
                    if g:
                        b, p = divmod(v, 4)
                        if g.fixed and g.n == 0 and v == 0:
                            pe.wait_ge(s_ones, 2)
                        if v == 0:
                            taken(pe, slot_before(sl), (RP + 1) % STEPS, LATE)
                        if p == 0:
                            if not (g.fixed and g.n == 0 and b == 0):
                                pe.wait_ge(s_o, g.n * GB + b)
                            mm(PS[:, 2, :], zero_bf[:, 0:P], zero_bf[:, :], start=True, stop=False,
                               skip_group_check=True)
                        pe.wait_ge(s_pt, g.n * NU + 4 * b + min(p + 1, 3) + 1)
                        for kb in (2 * p, 2 * p + 1):
                            nq = min(3, NQ - kb)
                            for a in range(HG):
                                pt = probsT[:, b, a, :, :, :].rearrange("p t c q -> p (t c) q")
                                r0, c0 = 64 * (a % 2), T * (a // 2) + Q * kb
                                ins = mm(PS[r0:r0 + 64, 2, c0:c0 + Q * nq],
                                         v_bd[:, g.par, b * NQ + kb, a, :, :].rearrange("p k f -> p (k f)"),
                                         pt[:, 3 * kb + 2:3 * kb + 2 + 2 * nq - 1:2, :],
                                         start=False, stop=(kb == NQ - 1), skip_group_check=True)
                        if p == 3:
                            ins.then_inc(s_o_ps, 1)

                    def free(place):
                        use = shared_use(sl, s, place)
                        if not (sl.fixed and use.before == 0):
                            pe.wait_ge(s_taken[use.bank], use.before)
                        return use.bank, PS[:, RING[use.bank], :]

                    def keys(b):
                        g, _ = at(sl, s, KP[b])
                        if g:
                            side, bank = free(KEY_PLACE[b])
                            r = slice(T * b, T * b + T)
                            exact3(bank[:, 0:T], *w2(WK), xT_hi[:, r], xT_lo[:, r]).then_inc(s_filled[side], 1)

                    keys(0)
                    g, _ = at(sl, s, VP)
                    if g:
                        side, bank = free(EARLY)
                        for n in range(NT):
                            r = slice(P * n, P * n + P)
                            ins = exact3(bank[:, r], xT_hi[:, r], xT_lo[:, r], *w2(WV))
                        ins.then_inc(s_filled[side], 1)

                    def values(place, a):
                        side, bank = free(place)
                        if a == 0:
                            taken(pe, sl, VP % STEPS, EARLY)
                        mm(bank, spreadq[:, a, :], v_hi[:, :, :], start=True, stop=False)
                        mm(bank, spreadq[:, a, :], v_lo[:, :, :], start=False, stop=True).then_inc(s_filled[side], 1)

                    g, half = at(sl, s, RP, 1, 2)
                    if g:
                        values(EARLY, 2 * half)
                    g, _ = at(sl, s, LG)
                    if g:
                        side, bank = free(EARLY)
                        taken(pe, slot_before(sl), (XT2 + 4) % STEPS, LATE)
                        for n in range(NT):
                            r = slice(P * n, P * n + P)
                            ins = exact3(bank[:, E * n:E * n + E], x2_hi[:, g.par, r], x2_lo[:, g.par, r],
                                         *w2(GK, E))
                        ins.then_inc(s_filled[side], 1)

                    g, _ = at(sl, s, YT)
                    if g:
                        side, bank = free(EARLY)
                        pe.wait_ge(s_y, g.n + 1)
                        for n in range(NT):
                            ins = nc.tensor.transpose(bank[:, P * n:P * n + P], y_f[:, P * n:P * n + P], ident)
                        ins.then_inc(s_filled[side], 1)

                    g, k = at(sl, s, FF, 1, NP)
                    if g:
                        gate_up(g, k, k + 1)

                    g, u = at(sl, s, SC, 1, NU)
                    if g:
                        if u == 0:
                            pe.wait_ge(s_q_hi, g.n * GB + 1)
                            pe.wait_ge(s_q_lo, g.n * 8 + 4)
                            pe.wait_ge(s_k_hi, g.n * GB + 1)
                            pe.wait_ge(s_k_lo, HG * (g.n * GB + 1))
                        if u == NU // 2:
                            pe.wait_ge(s_q_hi, g.n * GB + 2)
                            pe.wait_ge(s_q_lo, g.n * 8 + 8)
                            pe.wait_ge(s_k_hi, g.n * GB + 2)
                            pe.wait_ge(s_k_lo, HG * (g.n * GB + 2))
                        j0 = Q if u % 4 == 0 else 0
                        for tt in range(2):
                            if not (g.fixed and g.n == 0 and u == 0):
                                pe.wait_ge(s_p, 2 * (g.n * NU + u) + tt - 1)
                            t = 2 * (u % 4) + tt
                            dst = PS[:, tt, 0:HG * KW].rearrange("p (g k) -> p g k", g=HG)
                            mm(dst[:, :, j0:KW], ident4[:, :],
                               band[:, int(t == 0), j0:KW].unsqueeze(1).broadcast_to([P, HG, KW - j0]),
                               start=True, stop=False, skip_group_check=True)
                            nk = min(KW, (t + 1) * Q)
                            q1 = (u // 4) * T + (t + 1) * Q
                            for ql, kl in ((q_hi, k_hi), (q_lo, k_hi), (q_hi, k_lo)):
                                ins = mm(dst[:, :, KW - nk:KW],
                                         ql[:, q1 // Q - 1, :, :].rearrange("p v q -> p (v q)"),
                                         kl[:, :, q1 - nk:q1], start=False, stop=(kl is k_lo), skip_group_check=True)
                            ins.then_inc(s_s, 1)

                    g, b = at(sl, s, OT, 4, GB)
                    if g:
                        side, bank = free(POST)
                        pe.wait_ge(s_o, g.n * GB + b + 1)
                        for n in range(4):
                            half, j = divmod(n, 2)
                            ins = nc.tensor.transpose(bank[:, P * n:P * n + P], o_f[:, j, P * half:P * half + P], ident)
                        ins.then_inc(s_filled[side], 1)
                    g, b = at(sl, s, ON, 4, GB)
                    if g:
                        side, bank = free(POST)
                        taken(pe, sl, (s - 1) % STEPS, POST)
                        for half in range(2):
                            ins = nc.tensor.transpose(bank[:, P * half:P * half + P], o_n[:, half, :], ident)
                        ins.then_inc(s_filled[side], 1)
                    g, b = at(sl, s, OW, 4, GB)
                    if g:
                        side, bank = free(POST)
                        taken(pe, slot_before(sl) if s == 0 else sl, (s - 1) % STEPS, POST)
                        for half in range(2):
                            r = slice(P * half, P * half + P)
                            ins = exact3(bank[:, r], oT_hi[:, r], oT_lo[:, r], *w2(WO))
                        ins.then_inc(s_filled[side], 1)
                    g, _ = at(sl, s, CT)
                    if g:
                        side, bank = free(WEIGHTS)
                        pe.wait_ge(s_cb, g.n + 1)
                        for n in range(NT):
                            ins = nc.tensor.transpose(bank[0:E, P * n:P * n + P], comb[:, n, :], ident)
                        ins.then_inc(s_filled[side], 1)

                    g, _ = at(sl, s, SH)
                    if g:
                        gate_up(g, NP, 0)

                    g, half = at(sl, s, RP, 1, 2)
                    if g:
                        values(LATE, 2 * half + 1)
                    keys(1)
                    g, _ = at(sl, s, QP)
                    if g:
                        side, bank = free(LATE)
                        taken(pe, sl, XT % STEPS, LATE)
                        exact3(bank, *w2(WQ), xT_hi[:, :], xT_lo[:, :]).then_inc(s_filled[side], 1)
                    g, b = at(sl, s, XT2, 4, GB)
                    if g:
                        side, bank = free(LATE)
                        pe.wait_ge(s_xn2, g.n * GB + b + 1)
                        for n in range(2):
                            ins = nc.tensor.transpose(bank[:, P * n:P * n + P], xn2[:, n, :], ident)
                        ins.then_inc(s_filled[side], 1)
                    g, _ = at(sl, s, XT)
                    if g:
                        side, bank = free(LATE)
                        pe.wait_ge(s_xn1, g.n + 1)
                        for n in range(NT):
                            ins = nc.tensor.transpose(bank[:, P * n:P * n + P], X[:, g.par, n, :], ident)
                        ins.then_inc(s_filled[side], 1)
                    g, k = at(sl, s, DN, 1, NP)
                    if g:
                        if k == 0 and not (g.fixed and g.n == 0):
                            pe.wait_ge(s_y, g.n)
                        pe.wait_ge(s_h, g.n * NP + k + 1)
                        if k == 1:
                            pe.wait_ge(s_tu, g.n * NF + 1)
                            mm(PS[:, 7, :], wd[:, NP, :], hs[:, :], start=False, stop=False)
                        ins = mm(PS[:, 7, :], wd[:, k, :], hh[:, k % 2, :], start=(k == 0), stop=(k == NP - 1))
                        if k == NP - 1:
                            ins.then_inc(s_dn, 1)

            run_slots(pe, slot)


def kernel(**inputs):
    import numpy as np
    import concourse.bacc as _bacc
    from concourse import mybir as _mybir
    from concourse.bass_utils import run_bass_kernel_spmd as _run

    a = {k[3:]: np.asarray(v) for k, v in inputs.items()}
    both = [np.concatenate([a[f"ffn_w_{n}"].transpose(1, 0, 2).reshape(C, E * M), a[f"ffn_sw_{n}"]], axis=1)
            for n in ("gate", "up")]
    lanes = np.arange(P)

    cst = np.zeros((P, CONST_COLS), np.float32)

    def put(name, value):
        cst[:value.shape[0], CONST_AT[name]:CONST_AT[name] + CONSTS[name]] = value.reshape(value.shape[0], -1)

    put("ident", np.eye(P))
    put("headrow", (lanes[:, None] // D) % 4 == np.arange(4))
    put("grouprow", lanes[:, None] // 32 == np.arange(HG))
    put("headcol", lanes[:, None] // 32 == np.arange(32) // D)
    i, j = np.arange(Q)[:, None], np.arange(KW)
    seen = (j > i) & (j <= i + W)
    put("band", np.where(np.stack([seen, seen & (j >= W)], axis=1), 0.0, -1e30))
    put("spreadq", (lanes[:, None, None] == np.arange(4)[:, None] * 32 + lanes % 32))
    put("ident4", np.tile(np.eye(Q), 4))
    put("lower", np.tile((np.arange(N_GROUP)[None, :] < np.arange(N_GROUP)[:, None]).reshape(1, -1), (P, 1)))

    arrays = {
        "x": a["attn_x"].reshape(B * T, C),
        "w_att": np.concatenate([a[f"attn_W{n}"].T for n in "qkvo"] + [a["ffn_gate_kernel"]], axis=1),
        "gate_b": a["ffn_gate_bias"],
        "w_gu": np.concatenate(both, axis=1),
        "w_down": a["ffn_w_down"].reshape(E * M, C), "sw_down": a["ffn_sw_down"],
        "consts": cst,
    }
    arrays = {k: np.ascontiguousarray(v) for k, v in arrays.items()}
    nc = _bacc.Bacc("TRN2", target_bir_lowering=False, num_devices=1)
    args = [nc.dram_tensor(k, v.shape, _mybir.dt.from_np(v.dtype), kind="ExternalInput").ap()
            for k, v in arrays.items()]
    out = nc.dram_tensor("out", (B * T, C), _mybir.dt.float32, kind="ExternalOutput").ap()
    preln_block_kernel(nc, *args, out)
    r = _run(nc, [arrays], core_ids=[0])
    return r.results[0]["out"].reshape(B, T, C)
```
